# Optimizing a Trainium2 kernel written in Bass

```python
import numpy as np
import jax
import jax.numpy as jnp

def _softmax(x, axis=-1):
    return jax.nn.softmax(x, axis=axis)

def _gelu(x):
    return jax.nn.gelu(x, approximate=True)

def _silu(x):
    return jax.nn.silu(x)

def _sigmoid(x):
    return jax.nn.sigmoid(x)

def _layernorm(x, axis=-1, eps=1e-05):
    m = jnp.mean(x, axis=axis, keepdims=True)
    v = jnp.var(x, axis=axis, keepdims=True)
    return (x - m) / jnp.sqrt(v + eps)

def _scatter_add(tgt, idx, src, axis=0):
    return tgt.at[idx].add(src)

def _segment_sum(src, seg, n):
    return jax.ops.segment_sum(src, seg, n)
kernel_name = 'mk_prb_d1_jaxref_r2_e6e043'

def setup_inputs(seed: int=0):
    np.random.seed(seed)
    _w = jnp.asarray

    def _L0_attn_setup():
        import jax, jax.numpy as jnp
        import numpy as np
        BATCH, LENGTH = (2, 1024)
        D_INNER, D_STATE, DT_RANK = (512, 16, 64)
        DT_MIN, DT_MAX = (0.001, 0.1)
        key = jax.random.key(seed)
        k0, k1, k2, k3 = jax.random.split(key, 4)
        u = jax.random.normal(k0, (BATCH, LENGTH, D_INNER), dtype=jnp.float32)
        W_x = jax.random.normal(k1, (DT_RANK + 2 * D_STATE, D_INNER), dtype=jnp.float32) * 0.02
        W_dt = jax.random.normal(k2, (D_INNER, DT_RANK), dtype=jnp.float32) * DT_RANK ** (-0.5)
        dt = jnp.exp(jax.random.uniform(k3, (D_INNER,), dtype=jnp.float32) * (np.log(DT_MAX) - np.log(DT_MIN)) + np.log(DT_MIN))
        b_dt = dt + jnp.log(-jnp.expm1(-dt))
        log_A = jnp.log(jnp.tile(jnp.arange(1, D_STATE + 1, dtype=jnp.float32), (D_INNER, 1)))
        D_param = jnp.ones((D_INNER,), dtype=jnp.float32)
        return {'u': u, 'W_x': W_x, 'W_dt': W_dt, 'b_dt': b_dt, 'log_A': log_A, 'D_param': D_param}
    _L0_attn_in = _L0_attn_setup()

    def _L0_ffn_setup():
        import jax, jax.numpy as jnp
        import numpy as np
        FP8_E4M3_MAX = 448.0

        def fake_quant_fp8(t):
            amax = jnp.max(jnp.abs(t))
            scale = FP8_E4M3_MAX / jnp.maximum(amax, 1e-12)
            q = (t * scale).astype(jnp.float8_e4m3fn).astype(jnp.float32)
            return q / scale
        key = jax.random.key(seed)
        k1, k2, k3 = jax.random.split(key, 3)
        d_in, d_out = (512, 512)
        x = jax.random.normal(k1, (4, 4096, d_in), dtype=jnp.float32)
        weight = jax.random.normal(k2, (d_out, d_in), dtype=jnp.float32) * (1.0 / np.sqrt(d_in))
        bias = jax.random.normal(k3, (d_out,), dtype=jnp.float32) * 0.01
        return {'x': x, 'weight': weight, 'bias': bias}
    _L0_ffn_in = _L0_ffn_setup()
    _d = {'L0_attn_u': _L0_attn_in['u'], 'L0_attn_W_x': _L0_attn_in['W_x'], 'L0_attn_W_dt': _L0_attn_in['W_dt'], 'L0_attn_b_dt': _L0_attn_in['b_dt'], 'L0_attn_log_A': _L0_attn_in['log_A'], 'L0_attn_D_param': _L0_attn_in['D_param'], 'L0_ffn_weight': _L0_ffn_in['weight'], 'L0_ffn_bias': _L0_ffn_in['bias']}
    _x0 = _d['L0_attn_u']
    _d['L0_attn_u'] = jax.random.normal(jax.random.fold_in(jax.random.key(seed), 1), (32, 1024, 512), dtype=_x0.dtype)
    del _x0
    return _d

def reference(L0_attn_u, L0_attn_W_x, L0_attn_W_dt, L0_attn_b_dt, L0_attn_log_A, L0_attn_D_param, L0_ffn_weight, L0_ffn_bias):

    def _L0_attn_ref(u, W_x, W_dt, b_dt, log_A, D_param):
        import jax, jax.numpy as jnp
        import numpy as np
        BATCH, LENGTH = (2, 1024)
        D_INNER, D_STATE, DT_RANK = (512, 16, 64)
        DT_MIN, DT_MAX = (0.001, 0.1)
        x_dbl = u @ W_x.T
        delta_r, Bm, Cm = jnp.split(x_dbl, [DT_RANK, DT_RANK + D_STATE], axis=-1)
        delta = jax.nn.softplus(delta_r @ W_dt.T + b_dt)
        A = -jnp.exp(log_A)
        A_bar = jnp.exp(delta[..., None] * A)
        b_el = delta[..., None] * Bm[:, :, None, :] * u[..., None]

        def combine(e1, e2):
            a1, b1 = e1
            a2, b2 = e2
            return (a1 * a2, a2 * b1 + b2)
        _, h = jax.lax.associative_scan(combine, (A_bar, b_el), axis=1)
        y = jnp.einsum('bldn,bln->bld', h, Cm)
        return y + u * D_param

    def _L0_ffn_ref(x, weight, bias):
        import jax, jax.numpy as jnp
        import numpy as np
        FP8_E4M3_MAX = 448.0

        def fake_quant_fp8(t):
            amax = jnp.max(jnp.abs(t))
            scale = FP8_E4M3_MAX / jnp.maximum(amax, 1e-12)
            q = (t * scale).astype(jnp.float8_e4m3fn).astype(jnp.float32)
            return q / scale
        xq = fake_quant_fp8(x)
        wq = fake_quant_fp8(weight)
        return jnp.einsum('bsd,od->bso', xq, wq) + bias
    x = L0_attn_u
    xn = _layernorm(x, axis=-1)
    x = x + _L0_attn_ref(xn, L0_attn_W_x, L0_attn_W_dt, L0_attn_b_dt, L0_attn_log_A, L0_attn_D_param) + _L0_ffn_ref(xn, L0_ffn_weight, L0_ffn_bias)
    return x

_drawn_inputs = setup_inputs


def setup_inputs(seed=0):
    import zlib

    import numpy as np

    out = dict(_drawn_inputs(seed))
    spreads = {'L0_attn_D_param': (1.0, 0.2)}
    factors = {'L0_attn_W_dt': 5.469, 'L0_attn_b_dt': 3.731, 'L0_attn_log_A': 4.382, 'L0_ffn_bias': 8.0}
    for name, (base, spread) in spreads.items():
        noise = np.random.default_rng([zlib.crc32(name.encode()), seed]).standard_normal(out[name].shape)
        drawn = base * np.exp(spread * noise) if base else spread * noise
        out[name] = jnp.asarray(drawn.astype(out[name].dtype))
    for name, factor in factors.items():
        out[name] = (out[name] * factor).astype(out[name].dtype)
    return out
```

```python
from contextlib import ExitStack

import concourse.bass as bass
from concourse import mybir

F32 = mybir.dt.float32
F32R = mybir.dt.float32r
BF16 = mybir.dt.bfloat16
I32 = mybir.dt.int32
ALU = mybir.AluOpType
ACT = mybir.ActivationFunctionType
AX_X = mybir.AxisListType.X

P = 128
NC = 4
L = NC * P
D = 512
NS = 16
RANK = 64
BC0 = RANK
DIRECT = (3, 7, 11, 15)
TURNED = [n for n in range(NS) if n not in DIRECT]
NT = len(TURNED)
LAG = 2
EPS = 1e-5
FP8_MAX = 448.0
EXPONENT = 0x7F800000
ROUND = 1.5 * 2.0 ** 20
FP8_LEAST_NORMAL = 2.0 ** -6
NCREP = 4


def misc_slots():
    slots = {(n, c): [] for n in range(NS) for c in range(NC)}

    def put(n, c, name, kind):
        slots[(n, c)].append((name, kind))

    for n in range(NS):
        put(n, 0, f"crep{(n + 1) % NS}", "p" if n == NS - 1 else "m")
        if n + 1 in DIRECT:
            put(n, 1, f"brep{n + 1}", "m")
    for i, (n, c) in enumerate([(0, 2), (0, 3), (1, 2), (1, 3)]):
        put(n, c, f"ffn{i}", "e")
    for i, (n, c) in enumerate([(3, 2), (3, 3), (4, 1), (4, 2)]):
        put(n, c, f"yT{i}", "e")
    for i, (n, c) in enumerate([(5, 1), (5, 2), (5, 3), (6, 2)]):
        put(n, c, f"xnT{i}", "p")
    put(7, 1, "dbl", "p")
    put(8, 1, "BT", "p")
    for i, (n, c) in enumerate([(8, 2), (8, 3), (9, 1), (9, 2)]):
        put(n, c, f"pre{i}", "p")
    for i, (n, c) in enumerate([(14, 1), (14, 2), (14, 3), (15, 0)]):
        put(n, c, f"duT{i}", "p")
    return slots


SLOTS = misc_slots()
PROLOGUE = (["WxT", "WdtT", "wT0", "wT1", "wT2", "wT3", "amaxT", "amaxB"] + [f"xnT{i}" for i in range(4)] + ["dbl", "BT"]
            + [f"pre{i}" for i in range(4)] + [f"duT{i}" for i in range(4)] + ["crep0"])
EPILOGUE = [f"ffn{i}" for i in range(4)] + [f"yT{i}" for i in range(4)]


def ordered(kinds):
    return [name for n in range(NS) for c in range(NC) for name, kind in SLOTS[(n, c)] if kind in kinds]


BODY = {"first": ordered("mp"), "mid": ordered("emp"), "last": ordered("em")}


class MiscEvents:

    def __init__(self, chunks):
        self.chunks = chunks
        self.per = len(BODY["mid"])
        assert self.per % 2 == 0
        self.start = {"pro": 0, "first": len(PROLOGUE)}
        self.mid = len(PROLOGUE) + len(BODY["first"])
        self.start["mid"] = self.start["last"] = self.mid
        self.names = {"pro": PROLOGUE, "epi": EPILOGUE, **BODY}
        assert (self.per * (chunks - 2)) % 2 == 0
        self.start["epi"] = self.mid + len(BODY["last"])

    def at(self, kind, K, name):
        pos = self.start[kind] + self.names[kind].index(name)
        count = pos // 2 + 1
        if kind in ("mid", "last"):
            return pos % 2, (K - 1) * (self.per // 2) + count
        if kind == "epi":
            return pos % 2, (self.chunks - 2) * (self.per // 2) + count
        return pos % 2, count


def build(nc, u, W_x, W_dt, b_dt, log_A, D_param, weight, bias, out):
    batches, length, _ = u.shape
    halves = length // L
    assert halves == 2 and u.shape[2] == D
    chunks = batches * halves
    tiles = chunks * NC
    misc = MiscEvents(chunks)

    x_dram = u.rearrange("b (h i p) d -> (b h) p i d", h=halves, p=P)
    out_dram = out.rearrange("b (h i p) d -> (b h) p i d", h=halves, p=P)

    def chunk_of(dram, K):
        if isinstance(K, int):
            return dram[K]
        return dram[bass.ds(K, 1)].rearrange("o p i d -> p (o i) d")

    with ExitStack() as ctx:
        def sb(name, shape, dt=F32):
            return ctx.enter_context(nc.sbuf_tensor(name, shape, dt))

        def psum(name, shape, dt=F32):
            return ctx.enter_context(nc.psum_tensor(name, shape, dt))

        def sem(name):
            return ctx.enter_context(nc.semaphore(name))

        xt = sb("xt", [P, 2, NC, D])
        xnT = sb("xnT", [P, 2, NC, L])
        delta = sb("delta", [P, 2, NC, L])
        du = sb("du", [P, 2, NC, L])
        duT = sb("duT", [P, 2, NC, D])
        bchl = sb("bchl", [P, 2, L], F32R)
        BT = sb("BT", [P, 2, NC, NS])
        work = sb("work", [P, 4, NC, L])
        xn = expo = work[:, 0]
        scaled = logs = work[:, 1]
        yD = relu = work[:, 2]
        outt = rounder = onep = work[:, 3]
        xq = sb("xq", [P, NC, L], BF16)
        dbl = sb("dbl", [P, L])
        bT = sb("bT", [P, 2, NC, D])
        bdir = sb("bdir", [P, NC, L])
        avals = sb("avals", [P, NC, L])
        hbuf = sb("hbuf", [P, 2, NC, L])
        pbuf = sb("pbuf", [P, 2, NC, L])
        crep = sb("crep", [P, NCREP, L])
        state = sb("state", [P, NS, NC])
        ident = sb("ident", [P, P])
        pairs_r = sb("pairs_r", [P, 32], F32R)
        one_r = sb("one_r", [2, 2], F32R)
        WxT = sb("WxT", [P, NC, P])
        WdtT = sb("WdtT", [RANK, D])
        wq = sb("wq", [P, NC, D], BF16)
        Aneg = sb("Aneg", [P, NC, NS])
        bdt = sb("bdt", [P, NC])
        Dcol = sb("Dcol", [P, NC])
        bias_r = sb("bias_r", [2, D], F32R)
        rstd = sb("rstd", [P, tiles])
        nmr = sb("nmr", [P, tiles])
        amax2 = sb("amax2", [P, 8])
        scales = sb("scales", [P, 8])
        stats = bT[:, 0].rearrange("p i d -> p (i d)")[:, 0:tiles * 6].rearrange("p (t s) -> p t s", s=6)
        rowmax = bT[:, 1, 0, 0:tiles]
        rowmin = bT[:, 1, 0, tiles:2 * tiles]
        mean = bT[:, 1, 1, 0:tiles]
        var = bT[:, 1, 1, tiles:2 * tiles]
        tmp = bT[:, 1, 2, 0:tiles]
        tmp2 = bT[:, 1, 2, tiles:2 * tiles]
        w_in = xt[:, 0]
        ones = duT[:, 1, 0, 0:P]
        pairs = duT[:, 1, 3, 0:32]
        bias2 = duT[0:2, 1, 1]
        bias_hi = duT[0:2, 1, 2]
        Wx_in = hbuf[0:RANK + 2 * NS, 1, 0, :]
        Wdt_in = hbuf[:, 1, 1, 0:NC * RANK].rearrange("p (c r) -> p c r", c=NC)
        wTf = pbuf[:, 0]
        wround = pbuf[:, 1]

        Y = [psum(f"Y{c}", [P, L]) for c in range(NC)]
        BP = [psum(f"BP{j}", [P, L]) for j in range(2)]
        M = [psum(f"M{j}", [P, 512]) for j in range(2)]

        consts_loaded = sem("consts_loaded")
        stat_x = [sem(f"stat_x{j}") for j in range(4)]
        stat_used = sem("stat_used")
        zeroed = sem("zeroed")
        consts_ready = sem("consts_ready")
        A_exp = sem("A_exp")
        chain = sem("chain")
        std_asked = sem("std_asked")
        std_ready = sem("std_ready")
        rstd_ready = sem("rstd_ready")
        amax_ready = sem("amax_ready")
        amax_row = sem("amax_row")
        weights_ready = sem("weights_ready")
        scales_ready = sem("scales_ready")
        misc_ready = [sem(f"misc_ready{j}") for j in range(2)]
        misc_used = [sem(f"misc_used{j}") for j in range(2)]
        x_loaded = [sem(f"x_loaded{j}") for j in range(2)]
        x_used = sem("x_used")
        xn_ready = sem("xn_ready")
        xnT_ready = sem("xnT_ready")
        dbl_ready = sem("dbl_ready")
        lows_ready = sem("lows_ready")
        BT_ready = sem("BT_ready")
        relu_ready = sem("relu_ready")
        e_ready = sem("e_ready")
        logs_ready = sem("logs_ready")
        onep_ready = sem("onep_ready")
        sums_ready = sem("sums_ready")
        corr_ready = sem("corr_ready")
        delta_ready = sem("delta_ready")
        du_ready = sem("du_ready")
        duT_ready = sem("duT_ready")
        quant_steps = sem("quant_steps")
        shifted = sem("shifted")
        xq_ready = sem("xq_ready")
        bT_ready = sem("bT_ready")
        a_ready = sem("a_ready")
        b_ready = sem("b_ready")
        bdir_ready = sem("bdir_ready")
        scan_done = sem("scan_done")
        crep_ready = sem("crep_ready")
        prod_done = sem("prod_done")
        sum_done = sem("sum_done")
        y_taken = sem("y_taken")
        part_ready = sem("part_ready")
        out_ready = sem("out_ready")
        stored = sem("stored")

        block = ctx.enter_context(nc.Block())

        def wait(eng, s, value):
            if isinstance(value, int) and value <= 0:
                return
            eng.wait_ge(s, value)

        def for_chunks(eng, body):
            body("first", 0, 0)
            with eng.Fori(0, (chunks - 2) // 2) as i:
                body("mid", i * 2 + 1, 1)
                body("mid", i * 2 + 2, 0)
            body("last", chunks - 1, 1)

        def events(kind, n, c):
            return [(name, k) for name, k in SLOTS[(n, c)] if name in BODY[kind]
                    and not (k == "e" and kind == "first") and not (k == "p" and kind == "last")]

        def turned_count(K, n):
            return K * (NT * NC) + NC * len([m for m in TURNED if m < n])

        @block.sync
        def _(sp):
            sp.dma_start(w_in, weight.rearrange("(j p) d -> p j d", p=P)).then_inc(consts_loaded, 16)
            sp.dma_start(Wx_in, W_x).then_inc(consts_loaded, 16)
            sp.dma_start(Wdt_in, W_dt.rearrange("(c p) r -> p c r", p=P)).then_inc(consts_loaded, 16)
            sp.dma_start(Aneg[:, :, :], log_A.rearrange("(c p) n -> p c n", p=P)).then_inc(consts_loaded, 16)
            with nc.allow_non_contiguous_dma(reason="two vectors of 512 numbers, a column for each block"):
                sp.dma_start(bdt[:, :], b_dt.rearrange("(c p) -> p c", p=P)).then_inc(consts_loaded, 16)
                sp.dma_start(Dcol[:, :], D_param.rearrange("(c p) -> p c", p=P)).then_inc(consts_loaded, 16)
            for r in range(2):
                sp.dma_start(duT[r:r + 1, 1, 1], bias.rearrange("(o d) -> o d", o=1)).then_inc(consts_loaded, 16)
            for j in range(4):
                sp.dma_start(work[:, j], chunk_of(x_dram, j)).then_inc(stat_x[j], 16)
            with sp.Fori(1, chunks // 4) as g:
                for j in range(4):
                    sp.wait_ge(stat_used, g * 4 + (j - 3))
                    sp.dma_start(work[:, j], chunk_of(x_dram, g * 4 + j)).then_inc(stat_x[j], 16)
            sp.wait_ge(weights_ready, 1)
            sp.dma_start(xt[:, 0], chunk_of(x_dram, 0)).then_inc(x_loaded[0], 16)

            def body(kind, K, q):
                if kind != "last":
                    wait(sp, x_used, K)
                    sp.dma_start(xt[:, 1 - q], chunk_of(x_dram, K + 1)).then_inc(x_loaded[1 - q], 16)
                if kind != "first":
                    sp.wait_ge(out_ready, K)
                    sp.dma_start(chunk_of(out_dram, K - 1), outt).then_inc(stored, 16)

            for_chunks(sp, body)
            sp.wait_ge(out_ready, chunks)
            sp.dma_start(chunk_of(out_dram, chunks - 1), outt).then_inc(stored, 16)
            sp.wait_ge(stored, 16 * chunks)

        @block.gpsimd
        def _(pool):
            g = nc.gpsimd
            g.memset(ident[:, :], 0.0)
            g.memset(pairs, 0.0)
            g.memset(ones, 1.0).then_inc(zeroed, 1)
            pool.wait_ge(zeroed, 1)
            g.affine_select(out=ident[:, :], in_=ident[:, :], compare_op=ALU.not_equal, fill=1.0, base=0,
                            pattern=[[-1, P]], channel_multiplier=1)
            g.affine_select(out=pairs, in_=pairs, compare_op=ALU.not_equal, fill=1.0, base=-BC0,
                            pattern=[[-1, 32]], channel_multiplier=1).then_inc(zeroed, 1)
            pool.wait_ge(zeroed, 2)
            g.affine_select(out=pairs, in_=pairs, compare_op=ALU.not_equal, fill=1.0, base=-BC0 - 32,
                            pattern=[[-1, 32]], channel_multiplier=1).then_inc(consts_ready, 1)

            def correct(Q):
                pool.wait_ge(onep_ready, Q + 1)
                pool.wait_ge(logs_ready, Q + 1)
                g.tensor_tensor(expo, expo, onep, ALU.subtract).then_inc(corr_ready, 1)

            def add_delta(Q, q):
                pool.wait_ge(sums_ready, Q + 1)
                pool.wait_ge(corr_ready, Q + 1)
                g.tensor_tensor(delta[:, q], relu, expo, ALU.add).then_inc(delta_ready, 1)

            def times_x(Q, q):
                pool.wait_ge(delta_ready, Q + 1)
                g.tensor_tensor(du[:, q], delta[:, q], xnT[:, q], ALU.mult).then_inc(du_ready, 1)

            def round_up(Q):
                pool.wait_ge(quant_steps, 3 * Q + 3)
                g.tensor_tensor(scaled, scaled, rounder, ALU.add).then_inc(shifted, 1)

            def round_back(Q):
                pool.wait_ge(shifted, Q + 1)
                g.tensor_tensor(xq[:, :, :], scaled, rounder, ALU.subtract).then_inc(xq_ready, 1)

            correct(0)
            add_delta(0, 0)
            times_x(0, 0)

            def body(kind, K, q):
                for n in range(NS):
                    step = K * NS + n
                    pool.wait_ge(scan_done, K * (NS * NC) + NC * (n + 1))
                    pool.wait_ge(crep_ready, step + 1)
                    wait(pool, sum_done, step - 1)
                    last = g.tensor_tensor(pbuf[:, n % 2], hbuf[:, n % 2],
                                           crep[:, n % NCREP].unsqueeze(1).to_broadcast([P, NC, L]), ALU.mult)
                    if q == 0:
                        last = g.tensor_copy(state[:, n, :], hbuf[:, n % 2, :, L - 1])
                    last.then_inc(prod_done, 1)
                    if n == 7:
                        round_up(K)
                    if n == 8:
                        round_back(K)
                    if kind != "last":
                        if n == 11:
                            correct(K + 1)
                        if n == 12:
                            add_delta(K + 1, 1 - q)
                        if n == 13:
                            times_x(K + 1, 1 - q)

            for_chunks(pool, body)

        @block.scalar
        def _(act):
            a = nc.scalar

            def take(kind, K, name):
                bank, count = misc.at(kind, K, name)
                act.wait_ge(misc_ready[bank], count)
                return M[bank], misc_used[bank]

            def normalise(Q, q):
                act.wait_ge(x_loaded[q], Q * 8 + (16 - 8 * q))
                for i in range(NC):
                    t = Q * NC + i
                    col = slice(t, t + 1) if isinstance(t, int) else bass.ds(t, 1)
                    last = a.activation(xn[:, i], xt[:, q, i], ACT.Identity, bias=nmr[:, col], scale=rstd[:, col])
                last.then_inc(xn_ready, 1)

            def event(kind, K, name, Q, q):
                what, i = name.rstrip("0123456789"), int(name[len(name.rstrip("0123456789")):] or 0)
                if what not in ("crep", "xnT", "dbl", "BT", "pre", "duT"):
                    return
                if what == "pre" and i == 0:
                    pass
                bank, used = take(kind, K, name)
                if what == "crep":
                    wait(act, prod_done, Q * NS + i - NCREP + 1)
                    a.activation(crep[:, i % NCREP], bank[:, :], ACT.Copy).then_inc(crep_ready, 1)
                    act.wait_ge(crep_ready, Q * NS + i + 1)
                    act.sem_inc(used, 1)
                elif what == "xnT":
                    a.activation(xnT[:, q, i], bank[:, :], ACT.Copy).then_inc(xnT_ready, 1)
                    act.wait_ge(xnT_ready, Q * NC + i + 1)
                    act.sem_inc(used, 1)
                elif what == "dbl":
                    a.activation(dbl[:, :], bank[:, :], ACT.Copy)
                    a.activation(bchl[BC0:P, q], bank[BC0:P, :], ACT.Copy).then_inc(dbl_ready, 1)
                    act.wait_ge(dbl_ready, Q + 1)
                    act.sem_inc(used, 1)
                elif what == "BT":
                    a.activation(BT[:, q], bank[:, :].rearrange("p (i m) -> p i m", i=NC)[:, :, BC0:BC0 + NS],
                                 ACT.Copy).then_inc(BT_ready, 1)
                    act.wait_ge(BT_ready, Q + 1)
                    act.sem_inc(used, 1)
                elif what == "pre":
                    a.activation(expo[:, i], bank[:, :], ACT.Abs, bias=bdt[:, i:i + 1])
                    a.activation(relu[:, i], bank[:, :], ACT.Relu, bias=bdt[:, i:i + 1]).then_inc(relu_ready, 1)
                    act.wait_ge(relu_ready, Q * NC + i + 1)
                    act.sem_inc(used, 1)
                elif what == "duT":
                    a.activation(duT[:, q, i], bank[:, :], ACT.Copy).then_inc(duT_ready, 1)
                    act.wait_ge(duT_ready, Q * NC + i + 1)
                    act.sem_inc(used, 1)

            def exponential(Q):
                act.wait_ge(relu_ready, NC * Q + NC)
                a.activation(expo, expo, ACT.Exp, scale=-1.0).then_inc(e_ready, 1)

            def logarithm(Q):
                act.wait_ge(e_ready, Q + 1)
                wait(act, xq_ready, Q)
                a.activation(logs, expo, ACT.Ln, bias=1.0).then_inc(logs_ready, 1)

            def make_bT(Q, q, n, i):
                if n in DIRECT:
                    return
                s = Q * NT + TURNED.index(n)
                if i == 0:
                    wait(act, b_ready, (s - 1) * NC)
                    if n == 0:
                        act.wait_ge(BT_ready, Q + 1)
                if n == 0:
                    act.wait_ge(duT_ready, NC * Q + i + 1)
                ins = a.activation(bT[:, TURNED.index(n) % 2, i], duT[:, q, i], ACT.Copy, scale=BT[:, q, i, n:n + 1])
                if i == NC - 1:
                    ins.then_inc(bT_ready, 1)

            act.wait_ge(consts_loaded, 16 * 8)
            a.activation(Aneg[:, :, :], Aneg[:, :, :], ACT.Exp).then_inc(A_exp, 1)
            act.wait_ge(std_asked, 1)
            a.activation(tmp2, tmp, ACT.Sqrt).then_inc(std_ready, 1)
            act.wait_ge(scales_ready, 1)
            normalise(0, 0)
            for name in PROLOGUE[8:]:
                event("pro", 0, name, 0, 0)
                if name == "pre3":
                    exponential(0)
                    logarithm(0)
            for i in range(NC):
                make_bT(0, 0, 0, i)

            def body(kind, K, q):
                for n in range(NS):
                    for c in range(NC):
                        unit = K * (NS * NC) + n * NC + c
                        if n == 0 and c == 0:
                            act.wait_ge(delta_ready, K + 1)
                        wait(act, scan_done, unit - NC + 1)
                        a.activation(avals[:, c], delta[:, q, c], ACT.Exp, scale=Aneg[:, c, n:n + 1]).then_inc(a_ready, 1)
                        if kind != "last":
                            if (n, c) == (3, 0):
                                normalise(K + 1, 1 - q)
                            if (n, c) == (10, 0):
                                exponential(K + 1)
                            if (n, c) == (10, 2):
                                logarithm(K + 1)
                        for name, k in events(kind, n, c):
                            Q, r = (K, q) if k == "m" else (K + 1, 1 - q)
                            if k != "e":
                                event(kind, K, name, Q, r)
                        if n + 1 < NS:
                            make_bT(K, q, n + 1, c)
                        elif kind != "last":
                            make_bT(K + 1, 1 - q, 0, c)

            for_chunks(act, body)

        @block.vector
        def _(dve):
            v = nc.vector
            steps = [0]

            def link(ins):
                steps[0] += 1
                ins.then_inc(chain, 1)
                dve.wait_ge(chain, steps[0])

            def take(kind, K, name):
                bank, count = misc.at(kind, K, name)
                dve.wait_ge(misc_ready[bank], count)
                return M[bank], misc_used[bank]

            with dve.Fori(0, chunks // 4) as grp:
                for j in range(4):
                    dve.wait_ge(stat_x[j], grp * 16 + 16)
                    t = (grp * 4 + j) * NC
                    v.tensor_reduce(rowmax[:, bass.ds(t, NC)], work[:, j], AX_X, ALU.max)
                    v.tensor_reduce(rowmin[:, bass.ds(t, NC)], work[:, j], AX_X, ALU.min)
                    for i in range(NC):
                        last = v.bn_stats(stats[:, bass.ds(t + i, 1)].rearrange("p o s -> p (o s)"), work[:, j, i])
                    last.then_inc(stat_used, 1)
            dve.wait_ge(stat_used, chunks)
            half = D // 2
            link(v.tensor_tensor(mean, stats[:, :, 1], stats[:, :, 4], ALU.add))
            link(v.tensor_tensor(tmp, stats[:, :, 1], stats[:, :, 4], ALU.subtract))
            link(v.tensor_tensor(tmp, tmp, tmp, ALU.mult))
            link(v.tensor_tensor(var, stats[:, :, 2], stats[:, :, 5], ALU.add))
            link(v.tensor_scalar(var, var, 1.0 / D, None, ALU.mult))
            link(v.scalar_tensor_tensor(var, tmp, 0.25, var, ALU.mult, ALU.add))
            link(v.tensor_scalar(mean, mean, 0.5, None, ALU.mult))
            v.tensor_scalar(tmp, var, EPS, None, ALU.add).then_inc(std_asked, 1)
            dve.wait_ge(std_ready, 1)
            link(v.reciprocal(rstd[:, :], tmp2))
            link(v.tensor_tensor(tmp2, rstd[:, :], rstd[:, :], ALU.mult))
            link(v.tensor_tensor(tmp2, tmp2, tmp, ALU.mult))
            link(v.tensor_scalar(tmp2, tmp2, -0.5, 1.5, ALU.mult, ALU.add))
            link(v.tensor_tensor(rstd[:, :], rstd[:, :], tmp2, ALU.mult))
            link(v.scalar_tensor_tensor(nmr[:, :], mean, -1.0, rstd[:, :], ALU.mult, ALU.mult))
            link(v.tensor_tensor(rowmax, rowmax, mean, ALU.subtract))
            link(v.tensor_tensor(rowmin, mean, rowmin, ALU.subtract))
            link(v.tensor_tensor(rowmax, rowmax, rowmin, ALU.max))
            link(v.tensor_tensor(rowmax, rowmax, rstd[:, :], ALU.mult))
            link(v.tensor_reduce(amax2[:, 0:1], rowmax, AX_X, ALU.max))
            dve.wait_ge(consts_loaded, 16 * 8)
            link(v.tensor_reduce(amax2[:, 1:2], w_in.rearrange("p j d -> p (j d)"), AX_X, ALU.max))
            link(v.tensor_reduce(amax2[:, 2:3], w_in.rearrange("p j d -> p (j d)"), AX_X, ALU.min))
            link(v.tensor_scalar(amax2[:, 2:3], amax2[:, 2:3], -1.0, None, ALU.mult))
            v.tensor_tensor(amax2[:, 1:2], amax2[:, 1:2], amax2[:, 2:3], ALU.max).then_inc(amax_ready, 1)
            dve.wait_ge(consts_ready, 1)
            link(v.tensor_copy(pairs_r[:, :], pairs))
            link(v.tensor_copy(one_r[:, :], ones[0:2, 0:2]))
            dve.wait_ge(A_exp, 1)
            link(v.tensor_scalar(Aneg[:, :, :], Aneg[:, :, :], -1.0, None, ALU.mult))
            bank, used = take("pro", 0, "WxT")
            src = bank[:, 0:NC * 96].rearrange("p (c m) -> p c m", c=NC)
            v.tensor_copy(WxT[:, :, 0:96], src)
            link(v.tensor_copy(WxT[:, :, 96:P], src[:, :, RANK:96]))
            dve.sem_inc(used, 1)
            bank, used = take("pro", 0, "WdtT")
            link(v.tensor_copy(WdtT[:, :], bank[0:RANK, :]))
            dve.sem_inc(used, 1)
            for c in range(NC):
                bank, used = take("pro", 0, f"wT{c}")
                link(v.tensor_copy(wTf[:, c], bank[:, :]))
                dve.sem_inc(used, 1)
            bank, used = take("pro", 0, "amaxT")
            link(v.tensor_reduce(amax2[0:2, 4:5], bank[0:2, 0:P], AX_X, ALU.max))
            dve.sem_inc(used, 1)
            v.tensor_scalar(amax2[0:2, 6:8], ident[0:2, 0:2], amax2[0:2, 4:5], None, ALU.mult).then_inc(amax_row, 1)
            bank, used = take("pro", 0, "amaxB")
            link(v.tensor_scalar(scales[:, 0:2], bank[:, 0:2], 1e-12, None, ALU.max))
            dve.sem_inc(used, 1)
            link(v.reciprocal(scales[:, 2:4], scales[:, 0:2]))
            link(v.tensor_scalar(scales[:, 2:4], scales[:, 2:4], FP8_MAX, None, ALU.mult))
            link(v.tensor_tensor(scales[:, 4:5], scales[:, 2:3], scales[:, 3:4], ALU.mult))
            link(v.reciprocal(scales[:, 5:6], scales[:, 4:5]))
            link(v.tensor_scalar(bias2, bias2, scales[0:2, 4:5], None, ALU.mult))
            link(v.tensor_copy(bias_hi.bitcast(F32R), bias2))
            link(v.tensor_tensor(bias2, bias2, bias_hi, ALU.subtract))
            link(v.tensor_scalar(bias2, bias2, ident[0:2, 1:2], None, ALU.mult))
            link(v.scalar_tensor_tensor(bias_r[:, :], bias_hi, ident[0:2, 0:1], bias2,
                                        ALU.mult, ALU.add))
            link(v.tensor_scalar(wTf, wTf, scales[:, 3:4], None, ALU.mult))
            link(v.tensor_scalar(wround.bitcast(I32), wTf.bitcast(I32), EXPONENT, None, ALU.bitwise_and))
            link(v.tensor_scalar(wround, wround, FP8_LEAST_NORMAL, ROUND, ALU.max, ALU.mult))
            link(v.tensor_tensor(wTf, wTf, wround, ALU.add))
            link(v.tensor_tensor(wq[:, :, :], wTf, wround, ALU.subtract))
            dve.sem_inc(weights_ready, 1)
            dve.sem_inc(scales_ready, 1)

            def low_halves(Q, q):
                dve.wait_ge(dbl_ready, Q + 1)
                v.tensor_tensor(bchl[96:P, q], dbl[96:P, :], bchl[96:P, q].bitcast(F32),
                                ALU.subtract).then_inc(lows_ready, 1)

            def one_plus(Q):
                dve.wait_ge(e_ready, Q + 1)
                wait(dve, xq_ready, Q)
                v.tensor_scalar(onep, expo, 1.0, -1.0, ALU.add, ALU.add).then_inc(onep_ready, 1)

            def add_logs(Q):
                dve.wait_ge(logs_ready, Q + 1)
                v.tensor_tensor(relu, relu, logs, ALU.add).then_inc(sums_ready, 1)

            def quantise(Q, q):
                wait(dve, stored, 16 * Q)
                v.tensor_scalar(scaled, xnT[:, q], scales[:, 2:3], None, ALU.mult).then_inc(quant_steps, 1)
                dve.wait_ge(quant_steps, 3 * Q + 1)
                v.tensor_scalar(rounder.bitcast(I32), scaled.bitcast(I32), EXPONENT, None,
                                ALU.bitwise_and).then_inc(quant_steps, 1)
                dve.wait_ge(quant_steps, 3 * Q + 2)
                v.tensor_scalar(rounder, rounder, FP8_LEAST_NORMAL, ROUND, ALU.max, ALU.mult).then_inc(quant_steps, 1)

            def add_D(Q, q):
                dve.wait_ge(sum_done, Q * NS + NS)
                for c in range(NC):
                    v.scalar_tensor_tensor(yD[:, c], xnT[:, q, c], Dcol[:, c:c + 1], Y[c][:, :],
                                           ALU.mult, ALU.add).then_inc(y_taken, 1)

            def event(kind, K, name, Q, q):
                what, i = name.rstrip("0123456789"), int(name[len(name.rstrip("0123456789")):] or 0)
                if what == "brep":
                    bank, used = take(kind, K, name)
                    j = Q * len(DIRECT) + DIRECT.index(i) + 1
                    v.tensor_tensor(bdir[:, :, :], du[:, q], bank[:, :].unsqueeze(1).to_broadcast([P, NC, L]),
                                    ALU.mult).then_inc(bdir_ready, 1)
                    dve.wait_ge(bdir_ready, j)
                    dve.sem_inc(used, 1)
                elif what == "ffn":
                    bank, used = take(kind, K, name)
                    v.scalar_tensor_tensor(outt[:, i], bank[:, :], scales[:, 5:6], xt[:, q, i],
                                           ALU.mult, ALU.add).then_inc(part_ready, 1)
                    dve.wait_ge(part_ready, Q * NC + i + 1)
                    dve.sem_inc(used, 1)
                    if i == NC - 1:
                        dve.sem_inc(x_used, 1)
                elif what == "yT":
                    bank, used = take(kind, K, name)
                    ins = v.tensor_tensor(outt[:, i], outt[:, i], bank[:, :], ALU.add)
                    ins.then_inc(used, 1)
                    if i == NC - 1:
                        dve.wait_ge(used, misc.at(kind, K, name)[1])
                        dve.sem_inc(out_ready, 1)

            low_halves(0, 0)
            one_plus(0)
            add_logs(0)

            def body(kind, K, q):
                for n in range(NS):
                    if n == LAG and kind != "first":
                        add_D(K - 1, 1 - q)
                    wait(dve, prod_done, K * NS + n - 1)
                    for c in range(NC):
                        unit = K * (NS * NC) + n * NC + c
                        dve.wait_ge(a_ready, unit + 1)
                        if n in DIRECT:
                            if c == 0:
                                dve.wait_ge(bdir_ready, K * len(DIRECT) + DIRECT.index(n) + 1)
                            b = bdir[:, c]
                        else:
                            done = turned_count(K, n) + c + 1
                            dve.wait_ge(b_ready, done)
                            b = BP[c % 2][:, :]
                        initial = 0.0 if q == 0 else state[:, n, c:c + 1]
                        v.tensor_tensor_scan(hbuf[:, n % 2, c], avals[:, c], b, initial,
                                             ALU.mult, ALU.add).then_inc(scan_done, 1)
                        for name, k in events(kind, n, c):
                            Q, r = (K, q) if k == "m" else (K - 1, 1 - q)
                            if k != "p":
                                event(kind, K, name, Q, r)
                        if (n, c) == (6, 0):
                            quantise(K, q)
                        if kind != "last":
                            if (n, c) == (7, 3):
                                low_halves(K + 1, 1 - q)
                            if (n, c) == (10, 3):
                                one_plus(K + 1)
                            if (n, c) == (11, 1):
                                add_logs(K + 1)

            for_chunks(dve, body)
            add_D(chunks - 1, 1)
            for name in EPILOGUE:
                event("epi", 0, name, chunks - 1, 1)

        @block.tensor
        def _(pe):
            t = nc.tensor

            def free(kind, K, name):
                bank, count = misc.at(kind, K, name)
                wait(pe, misc_used[bank], count - 1)
                return M[bank], misc_ready[bank]

            def event(kind, K, name, Q, q):
                what, i = name.rstrip("0123456789"), int(name[len(name.rstrip("0123456789")):] or 0)
                bank, ready = free(kind, K, name)
                if what in ("crep", "brep"):
                    if what == "crep" and i == 0:
                        pe.wait_ge(lows_ready, Q + 1)
                    col = i + (NS if what == "crep" else 0)
                    last = t.matmul(bank[:, :], pairs_r[BC0:P, col:col + 1].to_broadcast([P - BC0, P]),
                                    bchl[BC0:P, q], start=True, stop=True)
                elif what == "xnT":
                    pe.wait_ge(xn_ready, Q + 1)
                    for j in range(NC):
                        last = t.transpose(bank[:, j * P:(j + 1) * P], xn[:, j, i * P:(i + 1) * P], ident[:, :])
                elif what == "dbl":
                    pe.wait_ge(xnT_ready, NC * Q + NC)
                    for c in range(NC):
                        last = t.matmul(bank[:, :], WxT[:, c], xnT[:, q, c], start=(c == 0), stop=(c == NC - 1))
                elif what == "BT":
                    pe.wait_ge(dbl_ready, Q + 1)
                    for j in range(NC):
                        last = t.transpose(bank[:, j * P:(j + 1) * P], dbl[:, j * P:(j + 1) * P], ident[:, :])
                elif what == "pre":
                    last = t.matmul(bank[:, :], WdtT[:, i * P:(i + 1) * P], dbl[0:RANK, :], start=True, stop=True)
                elif what == "duT":
                    pe.wait_ge(du_ready, Q + 1)
                    for c in range(NC):
                        last = t.transpose(bank[:, c * P:(c + 1) * P], du[:, q, c, i * P:(i + 1) * P], ident[:, :])
                elif what == "ffn":
                    pe.wait_ge(xq_ready, Q + 1)
                    for c in range(NC):
                        t.matmul(bank[:, :], xq[:, c, i * P:(i + 1) * P], wq[:, c], start=(c == 0), stop=False)
                    last = t.matmul(bank[:, :], one_r[:, 0:1].to_broadcast([2, P]), bias_r[:, :], start=False, stop=True)
                elif what == "yT":
                    pe.wait_ge(y_taken, NC * Q + NC)
                    for c in range(NC):
                        last = t.transpose(bank[:, c * P:(c + 1) * P], yD[:, c, i * P:(i + 1) * P], ident[:, :])
                last.then_inc(ready, 1)

            pe.wait_ge(consts_ready, 1)
            pe.wait_ge(consts_loaded, 16 * 8)
            bank, ready = free("pro", 0, "WxT")
            for c in range(NC):
                last = t.transpose(bank[:, c * 96:(c + 1) * 96], Wx_in[:, c * P:(c + 1) * P], ident[0:96, 0:96])
            last.then_inc(ready, 1)
            bank, ready = free("pro", 0, "WdtT")
            for c in range(NC):
                last = t.transpose(bank[0:RANK, c * P:(c + 1) * P], Wdt_in[:, c], ident[:, :])
            last.then_inc(ready, 1)
            for c in range(NC):
                bank, ready = free("pro", 0, f"wT{c}")
                for j in range(NC):
                    last = t.transpose(bank[:, j * P:(j + 1) * P], w_in[:, j, c * P:(c + 1) * P], ident[:, :])
                last.then_inc(ready, 1)
            bank, ready = free("pro", 0, "amaxT")
            pe.wait_ge(amax_ready, 1)
            t.transpose(bank[0:2, 0:P], amax2[:, 0:2], ident[:, :]).then_inc(ready, 1)
            bank, ready = free("pro", 0, "amaxB")
            pe.wait_ge(amax_row, 1)
            t.matmul(bank[:, 0:2], ones[0:2, :], amax2[0:2, 6:8], start=True, stop=True).then_inc(ready, 1)
            for name in PROLOGUE[8:]:
                event("pro", 0, name, 0, 0)

            def add_up(K, n, c):
                step = K * NS + n
                if c == 0:
                    pe.wait_ge(prod_done, step + 1)
                if n == 0:
                    wait(pe, y_taken, (K - 1) * NC + c + 1)
                ins = t.matmul(Y[c][:, :], ident[:, :], pbuf[:, n % 2, c], start=(n == 0), stop=(n == NS - 1))
                if c == NC - 1:
                    ins.then_inc(sum_done, 1)

            def body(kind, K, q):
                for n in range(NS):
                    for c in range(NC):
                        if n not in DIRECT:
                            s = TURNED.index(n)
                            if c == 0:
                                pe.wait_ge(bT_ready, K * NT + s + 1)
                            if c >= 2:
                                before = K * (NS * NC) + n * NC + c - 2
                            elif s:
                                before = K * (NS * NC) + TURNED[s - 1] * NC + c + 2
                            else:
                                before = (K - 1) * (NS * NC) + TURNED[-1] * NC + c + 2
                            wait(pe, scan_done, before + 1)
                            for j in range(NC):
                                last = t.transpose(BP[c % 2][:, j * P:(j + 1) * P],
                                                   bT[:, s % 2, j, c * P:(c + 1) * P], ident[:, :])
                            last.then_inc(b_ready, 1)
                        if n >= LAG:
                            add_up(K, n - LAG, c)
                        elif kind != "first":
                            add_up(K - 1, n - LAG + NS, c)
                        for name, k in events(kind, n, c):
                            Q, r = {"m": (K, q), "e": (K - 1, 1 - q), "p": (K + 1, 1 - q)}[k]
                            event(kind, K, name, Q, r)

            for_chunks(pe, body)
            for n in range(NS - LAG, NS):
                for c in range(NC):
                    add_up(chunks - 1, n, c)
            for name in EPILOGUE:
                event("epi", 0, name, chunks - 1, 1)


_INS = ["L0_attn_u", "L0_attn_W_x", "L0_attn_W_dt", "L0_attn_b_dt", "L0_attn_log_A", "L0_attn_D_param",
        "L0_ffn_weight", "L0_ffn_bias"]


def kernel(**inputs):
    import numpy as _np
    import concourse.bacc as _bacc
    from concourse import mybir as _mybir
    from concourse.bass_utils import run_bass_kernel_spmd as _run

    nc = _bacc.Bacc("TRN2", target_bir_lowering=False, num_devices=1)
    arrays, args = {}, []
    for name in _INS:
        a = _np.ascontiguousarray(inputs[name])
        arrays[f"in_{name}"] = a
        args.append(nc.dram_tensor(f"in_{name}", a.shape, _mybir.dt.from_np(a.dtype), kind="ExternalInput").ap())
    shape = inputs["L0_attn_u"].shape
    out = nc.dram_tensor("out_0", shape, _mybir.dt.float32, kind="ExternalOutput").ap()
    build(nc, *args, out)
    r = _run(nc, [arrays], core_ids=[0])
    return r.results[0]["out_0"]
```

```python
from contextlib import ExitStack

import concourse.bass as bass
from concourse import mybir

F32 = mybir.dt.float32
F32R = mybir.dt.float32r
BF16 = mybir.dt.bfloat16
I32 = mybir.dt.int32
ALU = mybir.AluOpType
ACT = mybir.ActivationFunctionType
AX_X = mybir.AxisListType.X

P = 128
NC = 4
L = NC * P
D = 512
NS = 16
RANK = 64
BC0 = RANK
DIRECT = (3, 7, 11, 15)
TURNED = [n for n in range(NS) if n not in DIRECT]
NT = len(TURNED)
LAG = 3
NH = 4
EPS = 1e-5
FP8_MAX = 448.0
EXPONENT = 0x7F800000
ROUND = 1.5 * 2.0 ** 20
FP8_LEAST_NORMAL = 2.0 ** -6
NCREP = 4


def misc_slots():
    slots = {(n, c): [] for n in range(NS) for c in range(NC)}

    def put(kind, name, places):
        for i, place in enumerate(places):
            slots[place].append((name if len(places) == 1 else f"{name}{i}", kind))

    for n in range(NS):
        put("p" if n == NS - 1 else "m", f"crep{(n + 1) % NS}", [(n, 0)])
        if n + 1 in DIRECT:
            put("m", f"brep{n + 1}", [(n, 1)])
    put("p", "xnT", [(3, 1), (3, 2), (3, 3), (4, 0)])
    put("e", "yT", [(4, 1), (4, 2), (4, 3), (5, 0)])
    put("p", "dbl", [(5, 0)])
    put("p", "pre", [(6, 2), (6, 3), (7, 1), (7, 2)])
    put("p", "BT", [(7, 3)])
    put("p", "duT", [(13, 1), (13, 2), (13, 3), (14, 0)])
    put("m", "ffn", [(14, 2), (14, 3), (15, 2), (15, 3)])
    return slots


SLOTS = misc_slots()
EARLY = ("crep", "brep")
ACT_LATE = 2
PROLOGUE = (["WxT", "WdtT", "wT0", "wT1", "wT2", "wT3", "amaxT", "amaxB"] + [f"xnT{i}" for i in range(NC)]
            + ["dbl", "BT"] + [f"pre{i}" for i in range(NC)] + [f"duT{i}" for i in range(NC)] + ["crep0"])
QUANTISE = [(5, 3), (6, 1), (6, 3)]
EPILOGUE = [f"yT{i}" for i in range(NC)]


def parts(name):
    what = name.rstrip("0123456789")
    return what, int(name[len(what):] or 0)


def ordered(kinds):
    return [name for n in range(NS) for c in range(NC) for name, kind in SLOTS[(n, c)] if kind in kinds]


BODY = {"first": ordered("mp"), "mid": ordered("emp"), "last": ordered("em")}


class MiscEvents:

    def __init__(self, chunks):
        self.chunks = chunks
        self.per = len(BODY["mid"])
        assert self.per % 2 == 0
        self.start = {"pro": 0, "first": len(PROLOGUE)}
        self.mid = len(PROLOGUE) + len(BODY["first"])
        self.start["mid"] = self.start["last"] = self.mid
        self.names = {"pro": PROLOGUE, "epi": EPILOGUE, **BODY}
        assert (self.per * (chunks - 2)) % 2 == 0
        self.start["epi"] = self.mid + len(BODY["last"])

    def at(self, kind, K, name):
        pos = self.start[kind] + self.names[kind].index(name)
        count = pos // 2 + 1
        if kind in ("mid", "last"):
            return pos % 2, (K - 1) * (self.per // 2) + count
        if kind == "epi":
            return pos % 2, (self.chunks - 2) * (self.per // 2) + count
        return pos % 2, count


def build(nc, u, W_x, W_dt, b_dt, log_A, D_param, weight, bias, out):
    batches, length, _ = u.shape
    halves = length // L
    assert halves == 2 and u.shape[2] == D
    chunks = batches * halves
    tiles = chunks * NC
    misc = MiscEvents(chunks)

    x_dram = u.rearrange("b (h i p) d -> (b h) p i d", h=halves, p=P)
    out_dram = out.rearrange("b (h i p) d -> (b h) p i d", h=halves, p=P)

    def chunk_of(dram, K):
        if isinstance(K, int):
            return dram[K]
        return dram[bass.ds(K, 1)].rearrange("o p i d -> p (o i) d")

    with ExitStack() as ctx:
        def sb(name, shape, dt=F32):
            return ctx.enter_context(nc.sbuf_tensor(name, shape, dt))

        def psum(name, shape, dt=F32):
            return ctx.enter_context(nc.psum_tensor(name, shape, dt))

        def sem(name):
            return ctx.enter_context(nc.semaphore(name))

        xt = sb("xt", [P, 2, NC, D])
        xnT = sb("xnT", [P, 2, NC, L])
        delta = sb("delta", [P, 2, NC, L])
        du = sb("du", [P, 2, NC, L])
        duT = sb("duT", [P, 2, NC, D])
        bchl = sb("bchl", [P, 2, L], F32R)
        BT = sb("BT", [P, 2, NC, NS])
        work = sb("work", [P, 4, NC, L])
        xn = expo = work[:, 0]
        scaled = logs = work[:, 1]
        yD = relu = work[:, 2]
        outt = rounder = onep = work[:, 3]
        xq = sb("xq", [P, NC, L], BF16)
        dbl = sb("dbl", [P, L])
        bT = sb("bT", [P, 2, NC, D])
        bdir = sb("bdir", [P, NC, L])
        avals = sb("avals", [P, NC, L])
        h = sb("h", [P, NH, NC, L])
        crep = sb("crep", [P, NCREP, L])
        state = sb("state", [P, NS, NC])
        one = sb("one", [P, NC])
        ident = sb("ident", [P, P])
        pairs_r = sb("pairs_r", [P, 32], F32R)
        one_r = sb("one_r", [2, 2], F32R)
        WxT = sb("WxT", [P, NC, P])
        WdtT = sb("WdtT", [RANK, D])
        wq = sb("wq", [P, NC, D], BF16)
        Aneg = sb("Aneg", [P, NC, NS])
        bdt = sb("bdt", [P, NC])
        Dcol = sb("Dcol", [P, NC])
        bias_r = sb("bias_r", [2, D], F32R)
        rstd = sb("rstd", [P, tiles])
        nmr = sb("nmr", [P, tiles])
        amax2 = sb("amax2", [P, 8])
        scales = sb("scales", [P, 8])
        stats = bT[:, 0].rearrange("p i d -> p (i d)")[:, 0:tiles * 6].rearrange("p (t s) -> p t s", s=6)
        rowmax = bT[:, 1, 0, 0:tiles]
        rowmin = bT[:, 1, 0, tiles:2 * tiles]
        mean = bT[:, 1, 1, 0:tiles]
        var = bT[:, 1, 1, tiles:2 * tiles]
        tmp = bT[:, 1, 2, 0:tiles]
        tmp2 = bT[:, 1, 2, tiles:2 * tiles]
        w_in = xt[:, 0]
        ones = duT[:, 1, 0, 0:P]
        pairs = duT[:, 1, 3, 0:32]
        bias2 = duT[0:2, 1, 1]
        bias_hi = duT[0:2, 1, 2]
        Wx_in = h[0:RANK + 2 * NS, 1, 0, :]
        Wdt_in = h[:, 1, 1, 0:NC * RANK].rearrange("p (c r) -> p c r", c=NC)
        wTf = h[:, 2]
        wround = h[:, 3]

        Y = [psum(f"Y{c}", [P, L]) for c in range(NC)]
        BP = [psum(f"BP{j}", [P, L]) for j in range(2)]
        M = [psum(f"M{j}", [P, 512]) for j in range(2)]

        consts_loaded = sem("consts_loaded")
        stat_x = [sem(f"stat_x{j}") for j in range(4)]
        stat_used = sem("stat_used")
        zeroed = sem("zeroed")
        consts_ready = sem("consts_ready")
        A_exp = sem("A_exp")
        chain = sem("chain")
        std_asked = sem("std_asked")
        std_ready = sem("std_ready")
        rstd_ready = sem("rstd_ready")
        amax_ready = sem("amax_ready")
        amax_row = sem("amax_row")
        weights_ready = sem("weights_ready")
        scales_ready = sem("scales_ready")
        misc_ready = [sem(f"misc_ready{j}") for j in range(2)]
        misc_used = [sem(f"misc_used{j}") for j in range(2)]
        x_loaded = [sem(f"x_loaded{j}") for j in range(2)]
        x_used = sem("x_used")
        xn_ready = sem("xn_ready")
        xnT_ready = sem("xnT_ready")
        dbl_ready = sem("dbl_ready")
        lows_ready = sem("lows_ready")
        BT_ready = sem("BT_ready")
        relu_ready = sem("relu_ready")
        e_ready = sem("e_ready")
        logs_ready = sem("logs_ready")
        onep_ready = sem("onep_ready")
        sums_ready = sem("sums_ready")
        corr_ready = sem("corr_ready")
        delta_ready = sem("delta_ready")
        du_ready = sem("du_ready")
        duT_ready = sem("duT_ready")
        quant_steps = sem("quant_steps")
        shifted = sem("shifted")
        xq_ready = sem("xq_ready")
        bT_ready = sem("bT_ready")
        a_ready = sem("a_ready")
        b_ready = sem("b_ready")
        bdir_ready = sem("bdir_ready")
        scan_done = sem("scan_done")
        crep_ready = sem("crep_ready")
        prod_done = sem("prod_done")
        state_saved = sem("state_saved")
        sum_done = sem("sum_done")
        y_taken = sem("y_taken")
        part_ready = sem("part_ready")
        out_ready = sem("out_ready")
        stored = sem("stored")

        block = ctx.enter_context(nc.Block())

        def wait(eng, s, value):
            if isinstance(value, int) and value <= 0:
                return
            eng.wait_ge(s, value)

        def for_chunks(eng, body):
            body("first", 0, 0)
            with eng.Fori(0, (chunks - 2) // 2) as i:
                body("mid", i * 2 + 1, 1)
                body("mid", i * 2 + 2, 0)
            body("last", chunks - 1, 1)

        def events(kind, n, c):
            return [(name, k) for name, k in SLOTS[(n, c)] if name in BODY[kind]
                    and not (k == "e" and kind == "first") and not (k == "p" and kind == "last")]

        def turned_count(K, n):
            return K * (NT * NC) + NC * len([m for m in TURNED if m < n])

        @block.sync
        def _(sp):
            sp.dma_start(w_in, weight.rearrange("(j p) d -> p j d", p=P)).then_inc(consts_loaded, 16)
            sp.dma_start(Wx_in, W_x).then_inc(consts_loaded, 16)
            sp.dma_start(Wdt_in, W_dt.rearrange("(c p) r -> p c r", p=P)).then_inc(consts_loaded, 16)
            sp.dma_start(Aneg[:, :, :], log_A.rearrange("(c p) n -> p c n", p=P)).then_inc(consts_loaded, 16)
            with nc.allow_non_contiguous_dma(reason="two vectors of 512 numbers, a column for each block"):
                sp.dma_start(bdt[:, :], b_dt.rearrange("(c p) -> p c", p=P)).then_inc(consts_loaded, 16)
                sp.dma_start(Dcol[:, :], D_param.rearrange("(c p) -> p c", p=P)).then_inc(consts_loaded, 16)
            for r in range(2):
                sp.dma_start(duT[r:r + 1, 1, 1], bias.rearrange("(o d) -> o d", o=1)).then_inc(consts_loaded, 16)
            for j in range(4):
                sp.dma_start(work[:, j], chunk_of(x_dram, j)).then_inc(stat_x[j], 16)
            with sp.Fori(1, chunks // 4) as g:
                for j in range(4):
                    sp.wait_ge(stat_used, g * 4 + (j - 3))
                    sp.dma_start(work[:, j], chunk_of(x_dram, g * 4 + j)).then_inc(stat_x[j], 16)
            sp.wait_ge(weights_ready, 1)
            sp.dma_start(xt[:, 0], chunk_of(x_dram, 0)).then_inc(x_loaded[0], 16)

            def body(kind, K, q):
                if kind != "last":
                    wait(sp, x_used, K)
                    sp.dma_start(xt[:, 1 - q], chunk_of(x_dram, K + 1)).then_inc(x_loaded[1 - q], 16)
                if kind != "first":
                    sp.wait_ge(out_ready, K)
                    sp.dma_start(chunk_of(out_dram, K - 1), outt).then_inc(stored, 16)

            for_chunks(sp, body)
            sp.wait_ge(out_ready, chunks)
            sp.dma_start(chunk_of(out_dram, chunks - 1), outt).then_inc(stored, 16)
            sp.wait_ge(stored, 16 * chunks)

        @block.gpsimd
        def _(pool):
            g = nc.gpsimd
            g.memset(ident[:, :], 0.0)
            g.memset(pairs, 0.0)
            g.memset(one[:, :], 1.0)
            g.memset(ones, 1.0).then_inc(zeroed, 1)
            pool.wait_ge(zeroed, 1)
            g.affine_select(out=ident[:, :], in_=ident[:, :], compare_op=ALU.not_equal, fill=1.0, base=0,
                            pattern=[[-1, P]], channel_multiplier=1)
            g.affine_select(out=pairs, in_=pairs, compare_op=ALU.not_equal, fill=1.0, base=-BC0,
                            pattern=[[-1, 32]], channel_multiplier=1).then_inc(zeroed, 1)
            pool.wait_ge(zeroed, 2)
            g.affine_select(out=pairs, in_=pairs, compare_op=ALU.not_equal, fill=1.0, base=-BC0 - 32,
                            pattern=[[-1, 32]], channel_multiplier=1).then_inc(consts_ready, 1)

            def correct(Q):
                pool.wait_ge(onep_ready, Q + 1)
                pool.wait_ge(logs_ready, Q + 1)
                g.tensor_tensor(expo, expo, onep, ALU.subtract).then_inc(corr_ready, 1)

            def add_delta(Q, q):
                pool.wait_ge(sums_ready, Q + 1)
                pool.wait_ge(corr_ready, Q + 1)
                g.tensor_tensor(delta[:, q], relu, expo, ALU.add).then_inc(delta_ready, 1)

            def times_x(Q, q):
                pool.wait_ge(delta_ready, Q + 1)
                g.tensor_tensor(du[:, q], delta[:, q], xnT[:, q], ALU.mult).then_inc(du_ready, 1)

            def round_up(Q):
                pool.wait_ge(quant_steps, 3 * Q + 3)
                g.tensor_tensor(scaled, scaled, rounder, ALU.add).then_inc(shifted, 1)

            def round_back(Q):
                pool.wait_ge(shifted, Q + 1)
                g.tensor_tensor(xq[:, :, :], scaled, rounder, ALU.subtract).then_inc(xq_ready, 1)

            correct(0)
            add_delta(0, 0)
            times_x(0, 0)

            def body(kind, K, q):
                for n in range(NS):
                    step = K * NS + n
                    pool.wait_ge(scan_done, K * (NS * NC) + NC * (n + 1))
                    pool.wait_ge(crep_ready, step + 1)
                    hn = h[:, n % NH]
                    if q == 0:
                        g.tensor_tensor(state[:, n, :], hn[:, :, L - 1], one[:, :], ALU.mult).then_inc(state_saved, 1)
                        saved = K * (NS // 2) + n + 1
                        pool.wait_ge(state_saved, saved)
                    g.tensor_tensor(hn, hn, crep[:, n % NCREP].unsqueeze(1).to_broadcast([P, NC, L]),
                                    ALU.mult).then_inc(prod_done, 1)
                    if n == 6:
                        round_up(K)
                    if n == 7:
                        round_back(K)
                    if kind != "last":
                        if n == 9:
                            correct(K + 1)
                        if n == 10:
                            add_delta(K + 1, 1 - q)
                        if n == 11:
                            times_x(K + 1, 1 - q)

            for_chunks(pool, body)

        @block.scalar
        def _(act):
            a = nc.scalar

            def take(kind, K, name):
                bank, count = misc.at(kind, K, name)
                act.wait_ge(misc_ready[bank], count)
                return M[bank], misc_used[bank]

            def normalise(Q, q, i):
                if i == 0:
                    act.wait_ge(x_loaded[q], Q * 8 + (16 - 8 * q))
                t = Q * NC + i
                col = slice(t, t + 1) if isinstance(t, int) else bass.ds(t, 1)
                ins = a.activation(xn[:, i], xt[:, q, i], ACT.Identity, bias=nmr[:, col], scale=rstd[:, col])
                if i == NC - 1:
                    ins.then_inc(xn_ready, 1)

            def event(kind, K, name, Q, q):
                what, i = parts(name)
                if what not in ("crep", "xnT", "dbl", "BT", "pre", "duT"):
                    return
                bank, used = take(kind, K, name)
                if what == "crep":
                    wait(act, prod_done, Q * NS + i - NCREP + 1)
                    a.activation(crep[:, i % NCREP], bank[:, :], ACT.Copy).then_inc(crep_ready, 1)
                    act.wait_ge(crep_ready, Q * NS + i + 1)
                    act.sem_inc(used, 1)
                elif what == "xnT":
                    wait(act, y_taken, (Q - 2) * NC + i + 1)
                    a.activation(xnT[:, q, i], bank[:, :], ACT.Copy).then_inc(xnT_ready, 1)
                    act.wait_ge(xnT_ready, Q * NC + i + 1)
                    act.sem_inc(used, 1)
                elif what == "dbl":
                    a.activation(dbl[:, :], bank[:, :], ACT.Copy)
                    a.activation(bchl[BC0:P, q], bank[BC0:P, :], ACT.Copy).then_inc(dbl_ready, 1)
                    act.wait_ge(dbl_ready, Q + 1)
                    act.sem_inc(used, 1)
                elif what == "BT":
                    a.activation(BT[:, q], bank[:, :].rearrange("p (i m) -> p i m", i=NC)[:, :, BC0:BC0 + NS],
                                 ACT.Copy).then_inc(BT_ready, 1)
                    act.wait_ge(BT_ready, Q + 1)
                    act.sem_inc(used, 1)
                elif what == "pre":
                    a.activation(expo[:, i], bank[:, :], ACT.Abs, bias=bdt[:, i:i + 1])
                    a.activation(relu[:, i], bank[:, :], ACT.Relu, bias=bdt[:, i:i + 1]).then_inc(relu_ready, 1)
                    act.wait_ge(relu_ready, Q * NC + i + 1)
                    act.sem_inc(used, 1)
                elif what == "duT":
                    a.activation(duT[:, q, i], bank[:, :], ACT.Copy).then_inc(duT_ready, 1)
                    act.wait_ge(duT_ready, Q * NC + i + 1)
                    act.sem_inc(used, 1)

            def exponential(Q):
                act.wait_ge(relu_ready, NC * Q + NC)
                a.activation(expo, expo, ACT.Exp, scale=-1.0).then_inc(e_ready, 1)

            def logarithm(Q):
                act.wait_ge(e_ready, Q + 1)
                wait(act, xq_ready, Q)
                a.activation(logs, expo, ACT.Ln, bias=1.0).then_inc(logs_ready, 1)

            def make_bT(Q, q, n, i):
                if n in DIRECT:
                    return
                s = Q * NT + TURNED.index(n)
                if i == 0:
                    wait(act, b_ready, (s - 1) * NC)
                    if n == 0:
                        act.wait_ge(BT_ready, Q + 1)
                if n == 0:
                    act.wait_ge(duT_ready, NC * Q + i + 1)
                ins = a.activation(bT[:, TURNED.index(n) % 2, i], duT[:, q, i], ACT.Copy, scale=BT[:, q, i, n:n + 1])
                if i == NC - 1:
                    ins.then_inc(bT_ready, 1)

            act.wait_ge(consts_loaded, 16 * 8)
            a.activation(Aneg[:, :, :], Aneg[:, :, :], ACT.Exp).then_inc(A_exp, 1)
            act.wait_ge(std_asked, 1)
            a.activation(tmp2, tmp, ACT.Sqrt).then_inc(std_ready, 1)

            act.wait_ge(scales_ready, 1)
            for i in range(NC):
                normalise(0, 0, i)
            for name in PROLOGUE[8:]:
                event("pro", 0, name, 0, 0)
                if name == "pre3":
                    exponential(0)
                    logarithm(0)
            for i in range(NC):
                make_bT(0, 0, 0, i)

            def body(kind, K, q):
                for n in range(NS):
                    for c in range(NC):
                        unit = K * (NS * NC) + n * NC + c
                        if n == 0 and c == 0:
                            act.wait_ge(delta_ready, K + 1)
                        wait(act, scan_done, unit - NC + 1)
                        a.activation(avals[:, c], delta[:, q, c], ACT.Exp, scale=Aneg[:, c, n:n + 1]).then_inc(a_ready, 1)
                        if n + 1 < NS:
                            make_bT(K, q, n + 1, c)
                        elif kind != "last":
                            make_bT(K + 1, 1 - q, 0, c)
                        slot = n * NC + c
                        for name, k in events(kind, *divmod(slot - ACT_LATE, NC)) if slot >= ACT_LATE else []:
                            Q, r = (K, q) if k == "m" else (K + 1, 1 - q)
                            if k != "e":
                                event(kind, K, name, Q, r)
                        if kind != "last":
                            if 5 <= slot < 5 + NC:
                                normalise(K + 1, 1 - q, slot - 5)
                            if (n, c) == (8, 1):
                                exponential(K + 1)
                            if (n, c) == (8, 2):
                                logarithm(K + 1)

            for_chunks(act, body)

        @block.vector
        def _(dve):
            v = nc.vector
            steps = [0]

            def link(ins):
                steps[0] += 1
                ins.then_inc(chain, 1)
                dve.wait_ge(chain, steps[0])

            def take(kind, K, name):
                bank, count = misc.at(kind, K, name)
                dve.wait_ge(misc_ready[bank], count)
                return M[bank], misc_used[bank]

            with dve.Fori(0, chunks // 4) as grp:
                for j in range(4):
                    dve.wait_ge(stat_x[j], grp * 16 + 16)
                    t = (grp * 4 + j) * NC
                    v.tensor_reduce(rowmax[:, bass.ds(t, NC)], work[:, j], AX_X, ALU.max)
                    v.tensor_reduce(rowmin[:, bass.ds(t, NC)], work[:, j], AX_X, ALU.min)
                    for i in range(NC):
                        last = v.bn_stats(stats[:, bass.ds(t + i, 1)].rearrange("p o s -> p (o s)"), work[:, j, i])
                    last.then_inc(stat_used, 1)
            dve.wait_ge(stat_used, chunks)
            half = D // 2
            link(v.tensor_tensor(mean, stats[:, :, 1], stats[:, :, 4], ALU.add))
            link(v.tensor_tensor(tmp, stats[:, :, 1], stats[:, :, 4], ALU.subtract))
            link(v.tensor_tensor(tmp, tmp, tmp, ALU.mult))
            link(v.tensor_tensor(var, stats[:, :, 2], stats[:, :, 5], ALU.add))
            link(v.tensor_scalar(var, var, 1.0 / D, None, ALU.mult))
            link(v.scalar_tensor_tensor(var, tmp, 0.25, var, ALU.mult, ALU.add))
            link(v.tensor_scalar(mean, mean, 0.5, None, ALU.mult))
            v.tensor_scalar(tmp, var, EPS, None, ALU.add).then_inc(std_asked, 1)
            dve.wait_ge(std_ready, 1)
            link(v.reciprocal(rstd[:, :], tmp2))
            link(v.tensor_tensor(tmp2, rstd[:, :], rstd[:, :], ALU.mult))
            link(v.tensor_tensor(tmp2, tmp2, tmp, ALU.mult))
            link(v.tensor_scalar(tmp2, tmp2, -0.5, 1.5, ALU.mult, ALU.add))
            link(v.tensor_tensor(rstd[:, :], rstd[:, :], tmp2, ALU.mult))
            link(v.scalar_tensor_tensor(nmr[:, :], mean, -1.0, rstd[:, :], ALU.mult, ALU.mult))
            link(v.tensor_tensor(rowmax, rowmax, mean, ALU.subtract))
            link(v.tensor_tensor(rowmin, mean, rowmin, ALU.subtract))
            link(v.tensor_tensor(rowmax, rowmax, rowmin, ALU.max))
            link(v.tensor_tensor(rowmax, rowmax, rstd[:, :], ALU.mult))
            link(v.tensor_reduce(amax2[:, 0:1], rowmax, AX_X, ALU.max))
            dve.wait_ge(consts_loaded, 16 * 8)
            link(v.tensor_reduce(amax2[:, 1:2], w_in.rearrange("p j d -> p (j d)"), AX_X, ALU.max))
            link(v.tensor_reduce(amax2[:, 2:3], w_in.rearrange("p j d -> p (j d)"), AX_X, ALU.min))
            link(v.tensor_scalar(amax2[:, 2:3], amax2[:, 2:3], -1.0, None, ALU.mult))
            v.tensor_tensor(amax2[:, 1:2], amax2[:, 1:2], amax2[:, 2:3], ALU.max).then_inc(amax_ready, 1)
            dve.wait_ge(consts_ready, 1)
            link(v.tensor_copy(pairs_r[:, :], pairs))
            link(v.tensor_copy(one_r[:, :], ones[0:2, 0:2]))
            dve.wait_ge(A_exp, 1)
            link(v.tensor_scalar(Aneg[:, :, :], Aneg[:, :, :], -1.0, None, ALU.mult))
            bank, used = take("pro", 0, "WxT")
            src = bank[:, 0:NC * 96].rearrange("p (c m) -> p c m", c=NC)
            v.tensor_copy(WxT[:, :, 0:96], src)
            link(v.tensor_copy(WxT[:, :, 96:P], src[:, :, RANK:96]))
            dve.sem_inc(used, 1)
            bank, used = take("pro", 0, "WdtT")
            link(v.tensor_copy(WdtT[:, :], bank[0:RANK, :]))
            dve.sem_inc(used, 1)
            for c in range(NC):
                bank, used = take("pro", 0, f"wT{c}")
                link(v.tensor_copy(wTf[:, c], bank[:, :]))
                dve.sem_inc(used, 1)
            bank, used = take("pro", 0, "amaxT")
            link(v.tensor_reduce(amax2[0:2, 4:5], bank[0:2, 0:P], AX_X, ALU.max))
            dve.sem_inc(used, 1)
            v.tensor_scalar(amax2[0:2, 6:8], ident[0:2, 0:2], amax2[0:2, 4:5], None, ALU.mult).then_inc(amax_row, 1)
            bank, used = take("pro", 0, "amaxB")
            link(v.tensor_scalar(scales[:, 0:2], bank[:, 0:2], 1e-12, None, ALU.max))
            dve.sem_inc(used, 1)
            link(v.reciprocal(scales[:, 2:4], scales[:, 0:2]))
            link(v.tensor_scalar(scales[:, 2:4], scales[:, 2:4], FP8_MAX, None, ALU.mult))
            link(v.tensor_tensor(scales[:, 4:5], scales[:, 2:3], scales[:, 3:4], ALU.mult))
            link(v.reciprocal(scales[:, 5:6], scales[:, 4:5]))
            link(v.tensor_scalar(bias2, bias2, scales[0:2, 4:5], None, ALU.mult))
            link(v.tensor_copy(bias_hi.bitcast(F32R), bias2))
            link(v.tensor_tensor(bias2, bias2, bias_hi, ALU.subtract))
            link(v.tensor_scalar(bias2, bias2, ident[0:2, 1:2], None, ALU.mult))
            link(v.scalar_tensor_tensor(bias_r[:, :], bias_hi, ident[0:2, 0:1], bias2,
                                        ALU.mult, ALU.add))
            link(v.tensor_scalar(wTf, wTf, scales[:, 3:4], None, ALU.mult))
            link(v.tensor_scalar(wround.bitcast(I32), wTf.bitcast(I32), EXPONENT, None, ALU.bitwise_and))
            link(v.tensor_scalar(wround, wround, FP8_LEAST_NORMAL, ROUND, ALU.max, ALU.mult))
            link(v.tensor_tensor(wTf, wTf, wround, ALU.add))
            link(v.tensor_tensor(wq[:, :, :], wTf, wround, ALU.subtract))
            dve.sem_inc(weights_ready, 1)
            dve.sem_inc(scales_ready, 1)

            def low_halves(Q, q):
                dve.wait_ge(dbl_ready, Q + 1)
                v.tensor_tensor(bchl[96:P, q], dbl[96:P, :], bchl[96:P, q].bitcast(F32),
                                ALU.subtract).then_inc(lows_ready, 1)

            def one_plus(Q):
                dve.wait_ge(e_ready, Q + 1)
                wait(dve, stored, 16 * (Q - 1))
                wait(dve, xq_ready, Q)
                v.tensor_scalar(onep, expo, 1.0, -1.0, ALU.add, ALU.add).then_inc(onep_ready, 1)

            def add_logs(Q):
                dve.wait_ge(logs_ready, Q + 1)
                v.tensor_tensor(relu, relu, logs, ALU.add).then_inc(sums_ready, 1)

            def quantise(Q, q, step):
                if step == 0:
                    ins = v.tensor_scalar(scaled, xnT[:, q], scales[:, 2:3], None, ALU.mult)
                elif step == 1:
                    wait(dve, stored, 16 * Q)
                    dve.wait_ge(quant_steps, 3 * Q + 1)
                    ins = v.tensor_scalar(rounder.bitcast(I32), scaled.bitcast(I32), EXPONENT, None, ALU.bitwise_and)
                else:
                    dve.wait_ge(quant_steps, 3 * Q + 2)
                    ins = v.tensor_scalar(rounder, rounder, FP8_LEAST_NORMAL, ROUND, ALU.max, ALU.mult)
                ins.then_inc(quant_steps, 1)

            def add_D(Q, q, c):
                dve.wait_ge(sum_done, (Q * NS + NS - 1) * NC + c + 1)
                v.scalar_tensor_tensor(yD[:, c], xnT[:, q, c], Dcol[:, c:c + 1], Y[c][:, :],
                                       ALU.mult, ALU.add).then_inc(y_taken, 1)

            def event(kind, K, name, Q, q):
                what, i = parts(name)
                if what == "brep":
                    bank, used = take(kind, K, name)
                    j = Q * len(DIRECT) + DIRECT.index(i) + 1
                    v.tensor_tensor(bdir[:, :, :], du[:, q], bank[:, :].unsqueeze(1).to_broadcast([P, NC, L]),
                                    ALU.mult).then_inc(bdir_ready, 1)
                    dve.wait_ge(bdir_ready, j)
                    dve.sem_inc(used, 1)
                elif what == "ffn":
                    bank, used = take(kind, K, name)
                    v.scalar_tensor_tensor(outt[:, i], bank[:, :], scales[:, 5:6], xt[:, q, i],
                                           ALU.mult, ALU.add).then_inc(part_ready, 1)
                    dve.wait_ge(part_ready, Q * NC + i + 1)
                    dve.sem_inc(used, 1)
                    if i == NC - 1:
                        dve.sem_inc(x_used, 1)
                elif what == "yT":
                    bank, used = take(kind, K, name)
                    ins = v.tensor_tensor(outt[:, i], outt[:, i], bank[:, :], ALU.add)
                    ins.then_inc(used, 1)
                    if i == NC - 1:
                        dve.wait_ge(used, misc.at(kind, K, name)[1])
                        dve.sem_inc(out_ready, 1)

            low_halves(0, 0)
            one_plus(0)
            add_logs(0)

            def body(kind, K, q):
                for n in range(NS):
                    for c in range(NC):
                        unit = K * (NS * NC) + n * NC + c
                        if n == LAG - 1 and kind != "first":
                            add_D(K - 1, 1 - q, c)
                        wait(dve, sum_done, unit - NH * NC + 1)
                        dve.wait_ge(a_ready, unit + 1)
                        if n in DIRECT:
                            if c == 0:
                                dve.wait_ge(bdir_ready, K * len(DIRECT) + DIRECT.index(n) + 1)
                            b = bdir[:, c]
                        else:
                            done = turned_count(K, n) + c + 1
                            dve.wait_ge(b_ready, done)
                            b = BP[c % 2][:, :]
                        initial = 0.0 if q == 0 else state[:, n, c:c + 1]
                        v.tensor_tensor_scan(h[:, n % NH, c], avals[:, c], b, initial,
                                             ALU.mult, ALU.add).then_inc(scan_done, 1)
                        for name, k in events(kind, n, c):
                            Q, r = (K, q) if k == "m" else (K - 1, 1 - q)
                            if k != "p":
                                event(kind, K, name, Q, r)
                        if (n, c) in QUANTISE:
                            quantise(K, q, QUANTISE.index((n, c)))
                        if kind != "last":
                            if (n, c) == (6, 2):
                                low_halves(K + 1, 1 - q)
                            if (n, c) == (8, 3):
                                one_plus(K + 1)
                            if (n, c) == (9, 0):
                                add_logs(K + 1)

            for_chunks(dve, body)
            for c in range(NC):
                add_D(chunks - 1, 1, c)
            for name in EPILOGUE:
                event("epi", 0, name, chunks - 1, 1)

        @block.tensor
        def _(pe):
            t = nc.tensor

            def free(kind, K, name):
                bank, count = misc.at(kind, K, name)
                wait(pe, misc_used[bank], count - 1)
                return M[bank], misc_ready[bank]

            def event(kind, K, name, Q, q):
                what, i = parts(name)
                if what == "dbl" and kind != "pro":
                    return
                bank, ready = free(kind, K, name)
                if what in ("crep", "brep"):
                    if what == "crep" and i == 0:
                        pe.wait_ge(lows_ready, Q + 1)
                    col = i + (NS if what == "crep" else 0)
                    last = t.matmul(bank[:, :], pairs_r[BC0:P, col:col + 1].to_broadcast([P - BC0, P]),
                                    bchl[BC0:P, q], start=True, stop=True)
                elif what == "xnT":
                    pe.wait_ge(xn_ready, Q + 1)
                    for j in range(NC):
                        last = t.transpose(bank[:, j * P:(j + 1) * P], xn[:, j, i * P:(i + 1) * P], ident[:, :])
                elif what == "dbl":
                    pe.wait_ge(xnT_ready, NC * Q + NC)
                    for c in range(NC):
                        last = t.matmul(bank[:, :], WxT[:, c], xnT[:, q, c], start=(c == 0), stop=(c == NC - 1))
                elif what == "BT":
                    pe.wait_ge(dbl_ready, Q + 1)
                    for j in range(NC):
                        last = t.transpose(bank[:, j * P:(j + 1) * P], dbl[:, j * P:(j + 1) * P], ident[:, :])
                elif what == "pre":
                    last = t.matmul(bank[:, :], WdtT[:, i * P:(i + 1) * P], dbl[0:RANK, :], start=True, stop=True)
                elif what == "duT":
                    pe.wait_ge(du_ready, Q + 1)
                    for c in range(NC):
                        last = t.transpose(bank[:, c * P:(c + 1) * P], du[:, q, c, i * P:(i + 1) * P], ident[:, :])
                elif what == "ffn":
                    pe.wait_ge(xq_ready, Q + 1)
                    for c in range(NC):
                        t.matmul(bank[:, :], xq[:, c, i * P:(i + 1) * P], wq[:, c], start=(c == 0), stop=False)
                    last = t.matmul(bank[:, :], one_r[:, 0:1].to_broadcast([2, P]), bias_r[:, :], start=False, stop=True)
                elif what == "yT":
                    pe.wait_ge(y_taken, NC * Q + NC)
                    for c in range(NC):
                        last = t.transpose(bank[:, c * P:(c + 1) * P], yD[:, c, i * P:(i + 1) * P], ident[:, :])
                last.then_inc(ready, 1)

            def projection(kind, K, Q, q, c):
                bank, ready = free(kind, K, "dbl")
                if c == 0:
                    pe.wait_ge(xnT_ready, NC * Q + NC)
                ins = t.matmul(bank[:, :], WxT[:, c], xnT[:, q, c], start=(c == 0), stop=(c == NC - 1))
                if c == NC - 1:
                    ins.then_inc(ready, 1)

            pe.wait_ge(consts_ready, 1)
            pe.wait_ge(consts_loaded, 16 * 8)
            bank, ready = free("pro", 0, "WxT")
            for c in range(NC):
                last = t.transpose(bank[:, c * 96:(c + 1) * 96], Wx_in[:, c * P:(c + 1) * P], ident[0:96, 0:96])
            last.then_inc(ready, 1)
            bank, ready = free("pro", 0, "WdtT")
            for c in range(NC):
                last = t.transpose(bank[0:RANK, c * P:(c + 1) * P], Wdt_in[:, c], ident[:, :])
            last.then_inc(ready, 1)
            for c in range(NC):
                bank, ready = free("pro", 0, f"wT{c}")
                for j in range(NC):
                    last = t.transpose(bank[:, j * P:(j + 1) * P], w_in[:, j, c * P:(c + 1) * P], ident[:, :])
                last.then_inc(ready, 1)
            bank, ready = free("pro", 0, "amaxT")
            pe.wait_ge(amax_ready, 1)
            t.transpose(bank[0:2, 0:P], amax2[:, 0:2], ident[:, :]).then_inc(ready, 1)
            bank, ready = free("pro", 0, "amaxB")
            pe.wait_ge(amax_row, 1)
            t.matmul(bank[:, 0:2], ones[0:2, :], amax2[0:2, 6:8], start=True, stop=True).then_inc(ready, 1)
            for name in PROLOGUE[8:]:
                event("pro", 0, name, 0, 0)

            def add_up(K, n, c):
                step = K * NS + n
                if c == 0:
                    pe.wait_ge(prod_done, step + 1)
                if n == 0:
                    wait(pe, y_taken, (K - 1) * NC + c + 1)
                t.matmul(Y[c][:, :], ident[:, :], h[:, n % NH, c], start=(n == 0),
                         stop=(n == NS - 1)).then_inc(sum_done, 1)

            def body(kind, K, q):
                for n in range(NS):
                    for c in range(NC):
                        now = [(name, *{"m": (K, q), "e": (K - 1, 1 - q), "p": (K + 1, 1 - q)}[k])
                               for name, k in events(kind, n, c)]
                        for name, Q, r in now:
                            if parts(name)[0] in EARLY:
                                event(kind, K, name, Q, r)
                        if n not in DIRECT:
                            s = TURNED.index(n)
                            if c == 0:
                                pe.wait_ge(bT_ready, K * NT + s + 1)
                            if c >= 2:
                                before = K * (NS * NC) + n * NC + c - 2
                            elif s:
                                before = K * (NS * NC) + TURNED[s - 1] * NC + c + 2
                            else:
                                before = (K - 1) * (NS * NC) + TURNED[-1] * NC + c + 2
                            wait(pe, scan_done, before + 1)
                            for j in range(NC):
                                last = t.transpose(BP[c % 2][:, j * P:(j + 1) * P],
                                                   bT[:, s % 2, j, c * P:(c + 1) * P], ident[:, :])
                            last.then_inc(b_ready, 1)
                        if n >= LAG:
                            add_up(K, n - LAG, c)
                        elif kind != "first":
                            add_up(K - 1, n - LAG + NS, c)
                        for name, Q, r in now:
                            if parts(name)[0] not in EARLY:
                                event(kind, K, name, Q, r)
                        if n == 5 and kind != "last":
                            projection(kind, K, K + 1, 1 - q, c)

            for_chunks(pe, body)
            for n in range(NS - LAG, NS):
                for c in range(NC):
                    add_up(chunks - 1, n, c)
            for name in EPILOGUE:
                event("epi", 0, name, chunks - 1, 1)


_INS = ["L0_attn_u", "L0_attn_W_x", "L0_attn_W_dt", "L0_attn_b_dt", "L0_attn_log_A", "L0_attn_D_param",
        "L0_ffn_weight", "L0_ffn_bias"]


def kernel(**inputs):
    import numpy as _np
    import concourse.bacc as _bacc
    from concourse import mybir as _mybir
    from concourse.bass_utils import run_bass_kernel_spmd as _run

    nc = _bacc.Bacc("TRN2", target_bir_lowering=False, num_devices=1)
    arrays, args = {}, []
    for name in _INS:
        a = _np.ascontiguousarray(inputs[name])
        arrays[f"in_{name}"] = a
        args.append(nc.dram_tensor(f"in_{name}", a.shape, _mybir.dt.from_np(a.dtype), kind="ExternalInput").ap())
    shape = inputs["L0_attn_u"].shape
    out = nc.dram_tensor("out_0", shape, _mybir.dt.float32, kind="ExternalOutput").ap()
    build(nc, *args, out)
    r = _run(nc, [arrays], core_ids=[0])
    return r.results[0]["out_0"]
```

```python
from contextlib import ExitStack

import concourse.bass as bass
from concourse import mybir

F32 = mybir.dt.float32
F32R = mybir.dt.float32r
BF16 = mybir.dt.bfloat16
U16 = mybir.dt.uint16
ALU = mybir.AluOpType
ACT = mybir.ActivationFunctionType
AX_X = mybir.AxisListType.X

P = 128
NC = 4
L = NC * P
D = 512
NS = 16
RANK = 64
BC0 = RANK
DIRECT = (4, 7, 9, 15)
TURNED = [n for n in range(NS) if n not in DIRECT]
NT = len(TURNED)
LAG = 3
NH = 4
EPS = 1e-5
FP8_MAX = 448.0
EXPONENT_HIGH = 0x7F80
ROUND = 1.5 * 2.0 ** 20
FP8_LEAST_NORMAL = 2.0 ** -6
NCREP = 4
OWN_STATS = 1

DBL = [(4, 1), (4, 2), (4, 3), (4, 3)]


def misc_slots():
    slots = {(n, c): [] for n in range(NS) for c in range(NC)}

    def put(kind, name, places):
        for i, place in enumerate(places):
            slots[place].append((name if len(places) == 1 else f"{name}{i}", kind))

    for n in range(NS):
        put("p" if n == NS - 1 else "m", f"crep{(n + 1) % NS}", [(n, 0)])
        if (n + 1) % NS in DIRECT:
            put("p" if n == NS - 1 else "m", f"brep{(n + 1) % NS}", [(n, 1)])
    put("p", "xnT", [(3, 0), (3, 1), (3, 2), (3, 3)])
    put("p", "dbl", [DBL[0]])
    put("e", "yT", [(6, 2), (7, 1), (7, 2), (7, 3)])
    put("p", "pre", [(5, 2), (6, 0), (6, 1), (6, 3)])
    put("p", "BT", [(9, 1)])
    put("p", "duT", [(14, 0), (14, 1), (14, 2), (14, 3)])
    put("m", "ffn", [(13, 1), (13, 3), (15, 1), (15, 3)])
    return slots


SLOTS = misc_slots()
EARLY = ("crep", "brep")
ACT_LATE = 2
PROLOGUE = (["WxT", "WdtT", "wT0", "wT1", "wT2", "wT3", "amaxT", "amaxB"] + [f"xnT{i}" for i in range(NC)]
            + ["dbl", "BT"] + [f"pre{i}" for i in range(NC)] + [f"duT{i}" for i in range(NC)]
            + ["crep0"] + ["brep0"] * (0 in DIRECT))
QUANTISE = [(0, 1), (0, 3), (1, 2)]
NORMALISE = [(1, 2), (1, 3), (2, 0), (2, 1)]
LOGARITHM = (8, 1)
LOW_HALVES, ONE_PLUS, ADD_LOGS = (5, 3), (7, 0), (8, 3)
PREPARATION = {7: [("correct", 0)], 8: [("correct", 1)], 9: [("add_delta", 0)],
               10: [("add_delta", 1), ("times_x", 0)], 11: [("times_x", 1)]}
QUANTISATION = {1: [("round_up", 0)], 2: [("round_up", 1)], 3: [("round_back", 0)], 4: [("round_back", 1)]}
EPILOGUE = [f"yT{i}" for i in range(NC)]


def parts(name):
    what = name.rstrip("0123456789")
    return what, int(name[len(what):] or 0)


def ordered(kinds):
    return [name for n in range(NS) for c in range(NC) for name, kind in SLOTS[(n, c)] if kind in kinds]


BODY = {"first": ordered("mp"), "mid": ordered("emp"), "last": ordered("em")}


class MiscEvents:

    def __init__(self, chunks):
        self.chunks = chunks
        self.names = {"pro": PROLOGUE, "epi": EPILOGUE, **BODY}

    def total(self, kind, bank):
        return (len(self.names[kind]) + 1 - bank) // 2

    def at(self, kind, K, name):
        index = self.names[kind].index(name)
        bank = index % 2
        count = index // 2 + 1
        if kind == "pro":
            return bank, count
        count += self.total("pro", bank)
        if kind == "first":
            return bank, count
        count += self.total("first", bank)
        if kind == "epi":
            return bank, count + (self.chunks - 2) * self.total("mid", bank) + self.total("last", bank)
        return bank, count + (K - 1) * self.total("mid", bank)


def build(nc, u, W_x, W_dt, b_dt, log_A, D_param, weight, bias, out):
    batches, length, _ = u.shape
    halves = length // L
    assert halves == 2 and u.shape[2] == D
    chunks = batches * halves
    tiles = chunks * NC
    misc = MiscEvents(chunks)

    x_dram = u.rearrange("b (h i p) d -> (b h) p i d", h=halves, p=P)
    out_dram = out.rearrange("b (h i p) d -> (b h) p i d", h=halves, p=P)

    def chunk_of(dram, K):
        if isinstance(K, int):
            return dram[K]
        return dram[bass.ds(K, 1)].rearrange("o p i d -> p (o i) d")

    with ExitStack() as ctx:
        def sb(name, shape, dt=F32):
            return ctx.enter_context(nc.sbuf_tensor(name, shape, dt))

        def psum(name, shape, dt=F32):
            return ctx.enter_context(nc.psum_tensor(name, shape, dt))

        def sem(name):
            return ctx.enter_context(nc.semaphore(name))

        xt = sb("xt", [P, 2, NC, D])
        xnT = sb("xnT", [P, 2, NC, L])
        delta = sb("delta", [P, 2, NC, L])
        du = sb("du", [P, 2, NC, L])
        duT = sb("duT", [P, 2, NC, D])
        bchl = sb("bchl", [P, 2, L], F32R)
        BT = sb("BT", [P, 2, NC, NS])
        work = sb("work", [P, 4, NC, L])
        xn = expo = work[:, 0]
        scaled = onep = work[:, 1]
        yD = work[:, 2]
        outt = work[:, 3]
        xq = sb("xq", [P, NC, L], BF16)
        dbl = sb("dbl", [P, L])
        bT = sb("bT", [P, 2, NC, D])
        bdir = sb("bdir", [P, NC, L])
        avals = sb("avals", [P, NC, L])
        h = sb("h", [P, NH, NC, L])
        crep = sb("crep", [P, NCREP, L])
        state = sb("state", [P, NS, NC])
        one = sb("one", [P, NC])
        ident = sb("ident", [P, P])
        pairs_r = sb("pairs_r", [P, 32], F32R)
        one_r = sb("one_r", [2, 2], F32R)
        WxT = sb("WxT", [P, NC, P])
        WdtT = sb("WdtT", [RANK, D])
        wq = sb("wq", [P, NC, D], BF16)
        Aneg = sb("Aneg", [P, NC, NS])
        bdt = sb("bdt", [P, NC])
        Dcol = sb("Dcol", [P, NC])
        bias_r = sb("bias_r", [2, D], F32R)
        rstd = sb("rstd", [P, tiles])
        nmr = sb("nmr", [P, tiles])
        amax2 = sb("amax2", [P, 8])
        scales = sb("scales", [P, 8])
        landing = [work[:, j] for j in range(4)]
        stats = bT[:, 0].rearrange("p i d -> p (i d)")[:, 0:tiles * 6].rearrange("p (t s) -> p t s", s=6)
        rowmax = bT[:, 1, 0, 0:tiles]
        rowmin = bT[:, 1, 0, tiles:2 * tiles]
        mean = bT[:, 1, 1, 0:tiles]
        var = bT[:, 1, 1, tiles:2 * tiles]
        tmp = bT[:, 1, 2, 0:tiles]
        tmp2 = bT[:, 1, 2, tiles:2 * tiles]
        negmean = bT[:, 1, 3, 0:tiles]
        groups = tiles // (4 * NC)

        def in_groups(t):
            return t.rearrange("p (g t) -> p g t", g=groups)

        top_square = in_groups(rowmax)[:, :, OWN_STATS * NC:]
        root = bT[:, 1, 3, tiles:tiles + groups * (4 - OWN_STATS) * NC].rearrange("p (g t) -> p g t", g=groups)
        w_in = bdir[:, :, :]
        ones = duT[:, 1, 0, 0:P]
        pairs = duT[:, 1, 3, 0:32]
        bias2 = duT[0:2, 1, 1]
        bias_hi = duT[0:2, 1, 2]
        Wx_in = h[0:RANK + 2 * NS, 1, 0, :]
        Wdt_in = h[:, 1, 1, 0:NC * RANK].rearrange("p (c r) -> p c r", c=NC)
        wTf = h[:, 2]
        unread = [du[:, q] for q in range(2)] + [xnT[:, 0]]
        squares = [delta[:, q] for q in range(2)] + [xnT[:, 1]]

        Y = [psum(f"Y{c}", [P, L]) for c in range(NC)]
        BP = [psum(f"BP{j}", [P, L]) for j in range(2)]
        M = [psum(f"M{j}", [P, 512]) for j in range(2)]

        consts_loaded = sem("consts_loaded")
        stat_x = [sem(f"stat_x{j}") for j in range(4)]
        stat_used = sem("stat_used")
        zeroed = sem("zeroed")
        consts_ready = sem("consts_ready")
        A_exp = sem("A_exp")
        chain = sem("chain")
        std_asked = sem("std_asked")
        std_ready = sem("std_ready")
        rstd_ready = sem("rstd_ready")
        amax_ready = sem("amax_ready")
        amax_row = sem("amax_row")
        mean_ready = sem("mean_ready")
        moments_ready = sem("moments_ready")
        misc_ready = [sem(f"misc_ready{j}") for j in range(2)]
        misc_used = [sem(f"misc_used{j}") for j in range(2)]
        x_loaded = [sem(f"x_loaded{j}") for j in range(2)]
        x_used = sem("x_used")
        xn_ready = sem("xn_ready")
        xnT_ready = sem("xnT_ready")
        dbl_ready = sem("dbl_ready")
        lows_ready = sem("lows_ready")
        BT_ready = sem("BT_ready")
        relu_ready = sem("relu_ready")
        e_ready = sem("e_ready")
        logs_ready = sem("logs_ready")
        onep_ready = sem("onep_ready")
        sums_ready = sem("sums_ready")
        corr_ready = sem("corr_ready")
        delta_ready = sem("delta_ready")
        du_ready = sem("du_ready")
        duT_ready = sem("duT_ready")
        quant_steps = sem("quant_steps")
        shifted = sem("shifted")
        xq_ready = sem("xq_ready")
        bT_ready = sem("bT_ready")
        a_ready = sem("a_ready")
        b_ready = sem("b_ready")
        bdir_ready = sem("bdir_ready")
        scan_done = sem("scan_done")
        crep_ready = sem("crep_ready")
        prod_done = sem("prod_done")
        state_saved = sem("state_saved")
        sum_done = sem("sum_done")
        y_taken = sem("y_taken")
        part_ready = sem("part_ready")
        out_ready = sem("out_ready")
        stored = sem("stored")

        block = ctx.enter_context(nc.Block())

        def slice_of(start, size):
            return slice(start, start + size) if isinstance(start, int) else bass.ds(start, size)

        def wait(eng, s, value):
            if isinstance(value, int) and value <= 0:
                return
            eng.wait_ge(s, value)

        def for_chunks(eng, body):
            body("first", 0, 0)
            with eng.Fori(0, (chunks - 2) // 2) as i:
                body("mid", i * 2 + 1, 1)
                body("mid", i * 2 + 2, 0)
            body("last", chunks - 1, 1)

        def events(kind, n, c):
            return [(name, k) for name, k in SLOTS[(n, c)] if name in BODY[kind]
                    and not (k == "e" and kind == "first") and not (k == "p" and kind == "last")]

        def turned_count(K, n):
            return K * (NT * NC) + NC * len([m for m in TURNED if m < n])

        @block.sync
        def _(sp):
            sp.dma_start(w_in, weight.rearrange("(j p) d -> p j d", p=P)).then_inc(consts_loaded, 16)
            sp.dma_start(Wx_in, W_x).then_inc(consts_loaded, 16)
            sp.dma_start(Wdt_in, W_dt.rearrange("(c p) r -> p c r", p=P)).then_inc(consts_loaded, 16)
            sp.dma_start(Aneg[:, :, :], log_A.rearrange("(c p) n -> p c n", p=P)).then_inc(consts_loaded, 16)
            with nc.allow_non_contiguous_dma(reason="two vectors of 512 numbers, a column for each block"):
                sp.dma_start(bdt[:, :], b_dt.rearrange("(c p) -> p c", p=P)).then_inc(consts_loaded, 16)
                sp.dma_start(Dcol[:, :], D_param.rearrange("(c p) -> p c", p=P)).then_inc(consts_loaded, 16)
            for r in range(2):
                sp.dma_start(duT[r:r + 1, 1, 1], bias.rearrange("(o d) -> o d", o=1)).then_inc(consts_loaded, 16)
            for j in range(4):
                sp.dma_start(landing[j], chunk_of(x_dram, j)).then_inc(stat_x[j], 16)
            with sp.Fori(1, chunks // 4) as g:
                for j in (1, 0, 2, 3):
                    if j < OWN_STATS:
                        sp.wait_ge(stat_used, g * 4 + (j - 3))
                    else:
                        sp.wait_ge(moments_ready, g * len(squares) + (j - 3))
                    sp.dma_start(landing[j], chunk_of(x_dram, g * 4 + j)).then_inc(stat_x[j], 16)
            sp.dma_start(xt[:, 0], chunk_of(x_dram, 0)).then_inc(x_loaded[0], 16)

            def body(kind, K, q):
                if kind != "last":
                    wait(sp, x_used, K)
                    sp.dma_start(xt[:, 1 - q], chunk_of(x_dram, K + 1)).then_inc(x_loaded[1 - q], 16)
                if kind != "first":
                    sp.wait_ge(out_ready, K)
                    sp.dma_start(chunk_of(out_dram, K - 1), outt).then_inc(stored, 16)

            for_chunks(sp, body)
            sp.wait_ge(out_ready, chunks)
            sp.dma_start(chunk_of(out_dram, chunks - 1), outt).then_inc(stored, 16)
            sp.wait_ge(stored, 16 * chunks)

        @block.gpsimd
        def _(pool):
            g = nc.gpsimd
            g.memset(ident[:, :], 0.0)
            g.memset(pairs, 0.0)
            g.memset(one[:, :], 1.0)
            g.memset(stats, 0.0)
            g.memset(ones, 1.0).then_inc(zeroed, 1)
            pool.wait_ge(zeroed, 1)
            g.affine_select(out=ident[:, :], in_=ident[:, :], compare_op=ALU.not_equal, fill=1.0, base=0,
                            pattern=[[-1, P]], channel_multiplier=1)
            g.affine_select(out=pairs, in_=pairs, compare_op=ALU.not_equal, fill=1.0, base=-BC0,
                            pattern=[[-1, 32]], channel_multiplier=1).then_inc(zeroed, 1)
            pool.wait_ge(zeroed, 2)
            g.affine_select(out=pairs, in_=pairs, compare_op=ALU.not_equal, fill=1.0, base=-BC0 - 32,
                            pattern=[[-1, 32]], channel_multiplier=1).then_inc(consts_ready, 1)

            halves_of = [slice(0, NC // 2), slice(NC // 2, NC)]

            def correct(Q, q, half):
                cs = halves_of[half]
                pool.wait_ge(onep_ready, Q + 1)
                g.tensor_tensor(onep[:, cs], expo[:, cs], onep[:, cs], ALU.subtract).then_inc(corr_ready, 1)

            def add_delta(Q, q, half):
                cs = halves_of[half]
                pool.wait_ge(sums_ready, Q + 1)
                pool.wait_ge(corr_ready, 2 * Q + half + 1)
                g.tensor_tensor(delta[:, q, cs], du[:, q, cs], onep[:, cs], ALU.add).then_inc(delta_ready, 1)

            def times_x(Q, q, half):
                cs = halves_of[half]
                pool.wait_ge(delta_ready, 2 * Q + half + 1)
                g.tensor_tensor(du[:, q, cs], delta[:, q, cs], xnT[:, q, cs], ALU.mult).then_inc(du_ready, 1)

            def round_up(Q, q, half):
                cs = halves_of[half]
                pool.wait_ge(quant_steps, 3 * Q + 3)
                g.tensor_tensor(scaled[:, cs], scaled[:, cs], xq[:, cs], ALU.add).then_inc(shifted, 1)

            def round_back(Q, q, half):
                cs = halves_of[half]
                pool.wait_ge(shifted, 2 * Q + half + 1)
                g.tensor_tensor(xq[:, cs], scaled[:, cs], xq[:, cs], ALU.subtract).then_inc(xq_ready, 1)

            stages = {stage.__name__: stage for stage in (correct, add_delta, times_x, round_up, round_back)}

            for stage in (correct, add_delta, times_x):
                for half in range(2):
                    stage(0, 0, half)

            def body(kind, K, q):
                for n in range(NS):
                    step = K * NS + n
                    pool.wait_ge(scan_done, K * (NS * NC) + NC * (n + 1))
                    pool.wait_ge(crep_ready, step + 1)
                    hn = h[:, n % NH]
                    if q == 0:
                        g.tensor_tensor(state[:, n, :], hn[:, :, L - 1], one[:, :], ALU.mult).then_inc(state_saved, 1)
                        saved = K * (NS // 2) + n + 1
                        pool.wait_ge(state_saved, saved)
                    g.tensor_tensor(hn, hn, crep[:, n % NCREP].unsqueeze(1).to_broadcast([P, NC, L]),
                                    ALU.mult).then_inc(prod_done, 1)
                    for stage, half in QUANTISATION.get(n, []):
                        stages[stage](K, q, half)
                    if kind != "last":
                        for stage, half in PREPARATION.get(n, []):
                            stages[stage](K + 1, 1 - q, half)

            for_chunks(pool, body)

        @block.scalar
        def _(act):
            a = nc.scalar

            def take(kind, K, name):
                bank, count = misc.at(kind, K, name)
                act.wait_ge(misc_ready[bank], count)
                return M[bank], misc_used[bank]

            def normalise(Q, q, i):
                if i == 0:
                    act.wait_ge(x_loaded[q], Q * 8 + (16 - 8 * q))
                t = Q * NC + i
                col = slice(t, t + 1) if isinstance(t, int) else bass.ds(t, 1)
                ins = a.activation(xn[:, i], xt[:, q, i], ACT.Identity, bias=nmr[:, col], scale=rstd[:, col])
                if i == NC - 1:
                    ins.then_inc(xn_ready, 1)

            def event(kind, K, name, Q, q):
                what, i = parts(name)
                if what not in ("crep", "xnT", "dbl", "BT", "pre", "duT"):
                    return
                bank, used = take(kind, K, name)
                if what == "crep":
                    wait(act, prod_done, Q * NS + i - NCREP + 1)
                    a.activation(crep[:, i % NCREP], bank[:, :], ACT.Copy).then_inc(crep_ready, 1)
                    act.wait_ge(crep_ready, Q * NS + i + 1)
                    act.sem_inc(used, 1)
                elif what == "xnT":
                    wait(act, y_taken, (Q - 2) * NC + i + 1)
                    a.activation(xnT[:, q, i], bank[:, :], ACT.Copy).then_inc(xnT_ready, 1)
                    act.wait_ge(xnT_ready, Q * NC + i + 1)
                    act.sem_inc(used, 1)
                elif what == "dbl":
                    a.activation(dbl[:, :], bank[:, :], ACT.Copy)
                    a.activation(bchl[BC0:P, q], bank[BC0:P, :], ACT.Copy).then_inc(dbl_ready, 1)
                    act.wait_ge(dbl_ready, Q + 1)
                    act.sem_inc(used, 1)
                elif what == "BT":
                    a.activation(BT[:, q], bank[:, :].rearrange("p (i m) -> p i m", i=NC)[:, :, BC0:BC0 + NS],
                                 ACT.Copy).then_inc(BT_ready, 1)
                    act.wait_ge(BT_ready, Q + 1)
                    act.sem_inc(used, 1)
                elif what == "pre":
                    a.activation(expo[:, i], bank[:, :], ACT.Abs, bias=bdt[:, i:i + 1])
                    a.activation(du[:, q, i], bank[:, :], ACT.Relu, bias=bdt[:, i:i + 1]).then_inc(relu_ready, 1)
                    act.wait_ge(relu_ready, Q * NC + i + 1)
                    act.sem_inc(used, 1)
                    a.activation(expo[:, i], expo[:, i], ACT.Exp, scale=-1.0).then_inc(e_ready, 1)
                elif what == "duT":
                    a.activation(duT[:, q, i], bank[:, :], ACT.Copy).then_inc(duT_ready, 1)
                    act.wait_ge(duT_ready, Q * NC + i + 1)
                    act.sem_inc(used, 1)


            def logarithm(Q, q):
                act.wait_ge(e_ready, NC * Q + NC)
                a.activation(delta[:, q], expo, ACT.Ln, bias=1.0).then_inc(logs_ready, 1)

            def make_bT(Q, q, n, i):
                if n in DIRECT:
                    return
                s = Q * NT + TURNED.index(n)
                if i == 0:
                    wait(act, b_ready, (s - 1) * NC)
                    if n == TURNED[0]:
                        act.wait_ge(BT_ready, Q + 1)
                if n == TURNED[0]:
                    act.wait_ge(duT_ready, NC * Q + i + 1)
                ins = a.activation(bT[:, TURNED.index(n) % 2, i], duT[:, q, i], ACT.Copy, scale=BT[:, q, i, n:n + 1])
                if i == NC - 1:
                    ins.then_inc(bT_ready, 1)

            act.wait_ge(consts_loaded, 16 * 8)
            a.activation(Aneg[:, :, :], Aneg[:, :, :], ACT.Exp).then_inc(A_exp, 1)
            act.wait_ge(zeroed, 1)

            def mean(grp, j):
                k = j - OWN_STATS
                act.wait_ge(stat_x[j], grp * 16 + 16)
                wait(act, mean_ready, (grp - 1) * len(unread) + k + 1)
                for i in range(NC):
                    row = slice_of((grp * 4 + j) * NC + i, 1)
                    ins = a.activation(unread[k][:, i], landing[j][:, i], ACT.Copy, scale=-1.0 / D,
                                       accum_out=negmean[:, row])
                ins.then_inc(mean_ready, 1)

            def moment(grp, j):
                k = j - OWN_STATS
                act.wait_ge(mean_ready, grp * len(unread) + k + 1)
                wait(act, moments_ready, (grp - 1) * len(squares) + k + 1)
                wait(act, stat_used, (grp - 1) * 4 + j + 1)
                for i in range(NC):
                    row = slice_of((grp * 4 + j) * NC + i, 1)
                    ins = a.activation(squares[k][:, i], landing[j][:, i], ACT.Square, bias=negmean[:, row],
                                       accum_out=stats[:, row, 2])
                ins.then_inc(moments_ready, 1)

            def moments(grp):
                for j in range(OWN_STATS, 4):
                    mean(grp, j)
                    if j > OWN_STATS:
                        moment(grp, j - 1)
                moment(grp, 3)

            moments(0)
            with act.Fori(1, chunks // 4) as grp:
                moments(grp)
            act.wait_ge(std_asked, 1)
            a.activation(tmp2, tmp, ACT.Sqrt).then_inc(std_ready, 1)
            a.activation(root, top_square, ACT.Sqrt).then_inc(std_ready, 1)

            act.wait_ge(rstd_ready, 1)
            for i in range(NC):
                normalise(0, 0, i)
            for name in PROLOGUE[8:]:
                event("pro", 0, name, 0, 0)
                if name == "pre3":
                    logarithm(0, 0)
            for i in range(NC):
                make_bT(0, 0, 0, i)

            def act_events(kind, slot):
                late = events(kind, *divmod(slot - ACT_LATE, NC)) if slot >= ACT_LATE else []
                late = [(name, k) for name, k in late if name != "dbl"]
                complete = kind != "last" and slot == DBL[-1][0] * NC + DBL[-1][1] + ACT_LATE
                return [("dbl", "p")] * complete + late

            def body(kind, K, q):
                for n in range(NS):
                    for c in range(NC):
                        unit = K * (NS * NC) + n * NC + c
                        if n == 0 and c == 0:
                            act.wait_ge(delta_ready, 2 * K + 2)
                        wait(act, scan_done, unit - NC + 1)
                        a.activation(avals[:, c], delta[:, q, c], ACT.Exp, scale=Aneg[:, c, n:n + 1]).then_inc(a_ready, 1)
                        if n + 1 < NS:
                            make_bT(K, q, n + 1, c)
                        elif kind != "last":
                            make_bT(K + 1, 1 - q, 0, c)
                        slot = n * NC + c
                        for name, k in act_events(kind, slot):
                            Q, r = (K, q) if k == "m" else (K + 1, 1 - q)
                            if k != "e":
                                event(kind, K, name, Q, r)
                        if kind != "last":
                            if (n, c) in NORMALISE:
                                normalise(K + 1, 1 - q, NORMALISE.index((n, c)))
                            if (n, c) == LOGARITHM:
                                logarithm(K + 1, 1 - q)

            for_chunks(act, body)

        @block.vector
        def _(dve):
            v = nc.vector
            steps = [0]

            def upper_half(t):
                return t.bitcast(U16).rearrange("p c (l two) -> p c l two", two=2)[:, :, :, 1]

            def link(ins):
                steps[0] += 1
                ins.then_inc(chain, 1)
                dve.wait_ge(chain, steps[0])

            def take(kind, K, name):
                bank, count = misc.at(kind, K, name)
                dve.wait_ge(misc_ready[bank], count)
                return M[bank], misc_used[bank]

            dve.wait_ge(consts_loaded, 16 * 8)
            link(v.tensor_reduce(amax2[:, 1:2], w_in.rearrange("p j d -> p (j d)"), AX_X, ALU.max))
            link(v.tensor_reduce(amax2[:, 2:3], w_in.rearrange("p j d -> p (j d)"), AX_X, ALU.min))
            link(v.tensor_scalar(amax2[:, 2:3], amax2[:, 2:3], -1.0, None, ALU.mult))
            link(v.tensor_tensor(amax2[:, 1:2], amax2[:, 1:2], amax2[:, 2:3], ALU.max))
            dve.wait_ge(consts_ready, 1)
            link(v.tensor_copy(pairs_r[:, :], pairs))
            link(v.tensor_copy(one_r[:, :], ones[0:2, 0:2]))
            dve.wait_ge(A_exp, 1)
            link(v.tensor_scalar(Aneg[:, :, :], Aneg[:, :, :], -1.0, None, ALU.mult))
            bank, used = take("pro", 0, "WxT")
            src = bank[:, 0:NC * 96].rearrange("p (c m) -> p c m", c=NC)
            v.tensor_copy(WxT[:, :, 0:96], src)
            link(v.tensor_copy(WxT[:, :, 96:P], src[:, :, RANK:96]))
            dve.sem_inc(used, 1)
            bank, used = take("pro", 0, "WdtT")
            link(v.tensor_copy(WdtT[:, :], bank[0:RANK, :]))
            dve.sem_inc(used, 1)
            for c in range(NC):
                bank, used = take("pro", 0, f"wT{c}")
                link(v.tensor_copy(wTf[:, c], bank[:, :]))
                dve.sem_inc(used, 1)
            dve.wait_ge(zeroed, 1)
            with dve.Fori(0, chunks // 4) as grp:
                for j in range(4):
                    t = (grp * 4 + j) * NC
                    if j < OWN_STATS:
                        dve.wait_ge(stat_x[j], grp * 16 + 16)
                        v.tensor_reduce(rowmin[:, bass.ds(t, NC)], landing[j], AX_X, ALU.min)
                        for i in range(NC):
                            v.bn_stats(stats[:, bass.ds(t + i, 1)].rearrange("p o s -> p (o s)"), landing[j][:, i])
                        from_rows = landing[j]
                    else:
                        dve.wait_ge(moments_ready, grp * len(squares) + (j - OWN_STATS + 1))
                        from_rows = squares[j - OWN_STATS]
                    v.tensor_reduce(rowmax[:, bass.ds(t, NC)], from_rows, AX_X, ALU.max).then_inc(stat_used, 1)
            dve.wait_ge(stat_used, chunks)
            by_scalar = slice(OWN_STATS * NC, None)
            for column in (1, 4):
                link(v.tensor_scalar(in_groups(stats[:, :, column])[:, :, by_scalar],
                                     in_groups(negmean)[:, :, by_scalar], -1.0, None, ALU.mult))
            link(v.tensor_tensor(mean, stats[:, :, 1], stats[:, :, 4], ALU.add))
            link(v.tensor_tensor(tmp, stats[:, :, 1], stats[:, :, 4], ALU.subtract))
            link(v.tensor_tensor(tmp, tmp, tmp, ALU.mult))
            link(v.tensor_tensor(var, stats[:, :, 2], stats[:, :, 5], ALU.add))
            link(v.tensor_scalar(var, var, 1.0 / D, None, ALU.mult))
            link(v.scalar_tensor_tensor(var, tmp, 0.25, var, ALU.mult, ALU.add))
            link(v.tensor_scalar(mean, mean, 0.5, None, ALU.mult))
            v.tensor_scalar(tmp, var, EPS, None, ALU.add).then_inc(std_asked, 1)
            dve.wait_ge(std_ready, 1)
            link(v.reciprocal(rstd[:, :], tmp2))
            link(v.tensor_tensor(tmp2, rstd[:, :], rstd[:, :], ALU.mult))
            link(v.tensor_tensor(tmp2, tmp2, tmp, ALU.mult))
            link(v.tensor_scalar(tmp2, tmp2, -0.5, 1.5, ALU.mult, ALU.add))
            link(v.tensor_tensor(rstd[:, :], rstd[:, :], tmp2, ALU.mult))
            link(v.scalar_tensor_tensor(nmr[:, :], mean, -1.0, rstd[:, :], ALU.mult, ALU.mult))
            dve.sem_inc(rstd_ready, 1)
            own = [in_groups(t)[:, :, 0:OWN_STATS * NC] for t in (rowmax, rowmin, mean)]
            link(v.tensor_tensor(own[0], own[0], own[2], ALU.subtract))
            link(v.tensor_tensor(own[1], own[2], own[1], ALU.subtract))
            link(v.tensor_tensor(own[0], own[0], own[1], ALU.max))
            dve.wait_ge(std_ready, 2)
            inverse = in_groups(rowmin)[:, :, OWN_STATS * NC:]
            link(v.tensor_scalar(root, root, 1e-30, None, ALU.max))
            link(v.reciprocal(inverse, root))
            link(v.tensor_tensor(top_square, top_square, inverse, ALU.mult))
            link(v.tensor_tensor(top_square, top_square, root, ALU.add))
            link(v.tensor_scalar(top_square, top_square, 0.5, None, ALU.mult))
            link(v.tensor_tensor(rowmax, rowmax, rstd[:, :], ALU.mult))
            v.tensor_reduce(amax2[:, 0:1], rowmax, AX_X, ALU.max).then_inc(amax_ready, 1)
            bank, used = take("pro", 0, "amaxT")
            link(v.tensor_reduce(amax2[0:2, 4:5], bank[0:2, 0:P], AX_X, ALU.max))
            dve.sem_inc(used, 1)
            v.tensor_scalar(amax2[0:2, 6:8], ident[0:2, 0:2], amax2[0:2, 4:5], None, ALU.mult).then_inc(amax_row, 1)
            bank, used = take("pro", 0, "amaxB")
            link(v.tensor_scalar(scales[:, 0:2], bank[:, 0:2], 1e-12, None, ALU.max))
            dve.sem_inc(used, 1)
            link(v.reciprocal(scales[:, 2:4], scales[:, 0:2]))
            link(v.tensor_scalar(scales[:, 2:4], scales[:, 2:4], FP8_MAX, None, ALU.mult))
            link(v.tensor_tensor(scales[:, 4:5], scales[:, 2:3], scales[:, 3:4], ALU.mult))
            link(v.reciprocal(scales[:, 5:6], scales[:, 4:5]))
            link(v.tensor_scalar(bias2, bias2, scales[0:2, 4:5], None, ALU.mult))
            link(v.tensor_copy(bias_hi.bitcast(F32R), bias2))
            link(v.tensor_tensor(bias2, bias2, bias_hi, ALU.subtract))
            link(v.tensor_scalar(bias2, bias2, ident[0:2, 1:2], None, ALU.mult))
            link(v.scalar_tensor_tensor(bias_r[:, :], bias_hi, ident[0:2, 0:1], bias2,
                                        ALU.mult, ALU.add))
            link(v.tensor_scalar(wTf, wTf, scales[:, 3:4], None, ALU.mult))
            link(v.tensor_scalar(wq[:, :, :].bitcast(U16), upper_half(wTf), EXPONENT_HIGH, None, ALU.bitwise_and))
            link(v.tensor_scalar(wq[:, :, :], wq[:, :, :], FP8_LEAST_NORMAL, ROUND, ALU.max, ALU.mult))
            link(v.tensor_tensor(wTf, wTf, wq[:, :, :], ALU.add))
            link(v.tensor_tensor(wq[:, :, :], wTf, wq[:, :, :], ALU.subtract))

            def low_halves(Q, q):
                dve.wait_ge(dbl_ready, Q + 1)
                v.tensor_tensor(bchl[96:P, q], dbl[96:P, :], bchl[96:P, q].bitcast(F32),
                                ALU.subtract).then_inc(lows_ready, 1)

            def one_plus(Q):
                dve.wait_ge(e_ready, NC * Q + NC)
                wait(dve, xq_ready, 2 * Q)
                v.tensor_scalar(onep, expo, 1.0, -1.0, ALU.add, ALU.add).then_inc(onep_ready, 1)

            def add_logs(Q, q):
                dve.wait_ge(logs_ready, Q + 1)
                v.tensor_tensor(du[:, q], du[:, q], delta[:, q], ALU.add).then_inc(sums_ready, 1)

            def quantise(Q, q, step):
                if step == 0:
                    dve.wait_ge(delta_ready, 2 * Q + 2)
                    ins = v.tensor_scalar(scaled, xnT[:, q], scales[:, 2:3], None, ALU.mult)
                elif step == 1:
                    dve.wait_ge(quant_steps, 3 * Q + 1)
                    ins = v.tensor_scalar(xq[:, :, :].bitcast(U16), upper_half(scaled),
                                          EXPONENT_HIGH, None, ALU.bitwise_and)
                else:
                    dve.wait_ge(quant_steps, 3 * Q + 2)
                    ins = v.tensor_scalar(xq[:, :, :], xq[:, :, :], FP8_LEAST_NORMAL, ROUND, ALU.max, ALU.mult)
                ins.then_inc(quant_steps, 1)

            def add_D(Q, q, c):
                dve.wait_ge(sum_done, (Q * NS + NS - 1) * NC + c + 1)
                v.scalar_tensor_tensor(yD[:, c], xnT[:, q, c], Dcol[:, c:c + 1], Y[c][:, :],
                                       ALU.mult, ALU.add).then_inc(y_taken, 1)

            def event(kind, K, name, Q, q):
                what, i = parts(name)
                if what == "brep":
                    if i == 0:
                        dve.wait_ge(du_ready, 2 * Q + 2)
                    bank, used = take(kind, K, name)
                    j = Q * len(DIRECT) + DIRECT.index(i) + 1
                    before = Q * NS + i - min((i - m) % NS or NS for m in DIRECT)
                    wait(dve, scan_done, (before + 1) * NC)
                    v.tensor_tensor(bdir[:, :, :], du[:, q], bank[:, :].unsqueeze(1).to_broadcast([P, NC, L]),
                                    ALU.mult).then_inc(bdir_ready, 1)
                    dve.wait_ge(bdir_ready, j)
                    dve.sem_inc(used, 1)
                elif what == "ffn":
                    if i == 0:
                        wait(dve, stored, 16 * Q)
                    bank, used = take(kind, K, name)
                    v.scalar_tensor_tensor(outt[:, i], bank[:, :], scales[:, 5:6], xt[:, q, i],
                                           ALU.mult, ALU.add).then_inc(part_ready, 1)
                    dve.wait_ge(part_ready, Q * NC + i + 1)
                    dve.sem_inc(used, 1)
                    if i == NC - 1:
                        dve.sem_inc(x_used, 1)
                elif what == "yT":
                    bank, used = take(kind, K, name)
                    ins = v.tensor_tensor(outt[:, i], outt[:, i], bank[:, :], ALU.add)
                    ins.then_inc(used, 1)
                    if i == NC - 1:
                        dve.wait_ge(used, misc.at(kind, K, name)[1])
                        dve.sem_inc(out_ready, 1)

            low_halves(0, 0)
            one_plus(0)
            add_logs(0, 0)
            if 0 in DIRECT:
                event("pro", 0, "brep0", 0, 0)

            def body(kind, K, q):
                for n in range(NS):
                    for c in range(NC):
                        unit = K * (NS * NC) + n * NC + c
                        if n == LAG - 1 and kind != "first":
                            add_D(K - 1, 1 - q, c)
                        wait(dve, sum_done, unit - NH * NC + 1)
                        dve.wait_ge(a_ready, unit + 1)
                        if n in DIRECT:
                            if c == 0:
                                dve.wait_ge(bdir_ready, K * len(DIRECT) + DIRECT.index(n) + 1)
                            b = bdir[:, c]
                        else:
                            done = turned_count(K, n) + c + 1
                            dve.wait_ge(b_ready, done)
                            b = BP[c % 2][:, :]
                        initial = 0.0 if q == 0 else state[:, n, c:c + 1]
                        v.tensor_tensor_scan(h[:, n % NH, c], avals[:, c], b, initial,
                                             ALU.mult, ALU.add).then_inc(scan_done, 1)
                        for name, k in events(kind, n, c):
                            Q, r = {"m": (K, q), "e": (K - 1, 1 - q), "p": (K + 1, 1 - q)}[k]
                            event(kind, K, name, Q, r)
                        if (n, c) in QUANTISE:
                            quantise(K, q, QUANTISE.index((n, c)))
                        if kind != "last":
                            if (n, c) == LOW_HALVES:
                                low_halves(K + 1, 1 - q)
                            if (n, c) == ONE_PLUS:
                                one_plus(K + 1)
                            if (n, c) == ADD_LOGS:
                                add_logs(K + 1, 1 - q)

            for_chunks(dve, body)
            for c in range(NC):
                add_D(chunks - 1, 1, c)
            for name in EPILOGUE:
                event("epi", 0, name, chunks - 1, 1)

        @block.tensor
        def _(pe):
            t = nc.tensor

            def free(kind, K, name):
                bank, count = misc.at(kind, K, name)
                wait(pe, misc_used[bank], count - 1)
                return M[bank], misc_ready[bank]

            def event(kind, K, name, Q, q):
                what, i = parts(name)
                if what == "dbl" and kind != "pro":
                    return
                bank, ready = free(kind, K, name)
                if what in ("crep", "brep"):
                    if what == "crep" and i == 0:
                        pe.wait_ge(lows_ready, Q + 1)
                    col = i + (NS if what == "crep" else 0)
                    last = t.matmul(bank[:, :], pairs_r[BC0:P, col:col + 1].to_broadcast([P - BC0, P]),
                                    bchl[BC0:P, q], start=True, stop=True)
                elif what == "xnT":
                    pe.wait_ge(xn_ready, Q + 1)
                    for j in range(NC):
                        last = t.transpose(bank[:, j * P:(j + 1) * P], xn[:, j, i * P:(i + 1) * P], ident[:, :])
                elif what == "dbl":
                    pe.wait_ge(xnT_ready, NC * Q + NC)
                    for c in range(NC):
                        last = t.matmul(bank[:, :], WxT[:, c], xnT[:, q, c], start=(c == 0), stop=(c == NC - 1))
                elif what == "BT":
                    pe.wait_ge(dbl_ready, Q + 1)
                    for j in range(NC):
                        last = t.transpose(bank[:, j * P:(j + 1) * P], dbl[:, j * P:(j + 1) * P], ident[:, :])
                elif what == "pre":
                    last = t.matmul(bank[:, :], WdtT[:, i * P:(i + 1) * P], dbl[0:RANK, :], start=True, stop=True)
                elif what == "duT":
                    pe.wait_ge(du_ready, 2 * Q + 2)
                    for c in range(NC):
                        last = t.transpose(bank[:, c * P:(c + 1) * P], du[:, q, c, i * P:(i + 1) * P], ident[:, :])
                elif what == "ffn":
                    pe.wait_ge(xq_ready, 2 * Q + 2)
                    for c in range(NC):
                        t.matmul(bank[:, :], xq[:, c, i * P:(i + 1) * P], wq[:, c], start=(c == 0), stop=False)
                    last = t.matmul(bank[:, :], one_r[:, 0:1].to_broadcast([2, P]), bias_r[:, :], start=False, stop=True)
                elif what == "yT":
                    pe.wait_ge(y_taken, NC * Q + NC)
                    for c in range(NC):
                        last = t.transpose(bank[:, c * P:(c + 1) * P], yD[:, c, i * P:(i + 1) * P], ident[:, :])
                last.then_inc(ready, 1)

            def projection(kind, K, Q, q, c):
                bank, ready = free(kind, K, "dbl")
                if c == 0:
                    pe.wait_ge(xnT_ready, NC * Q + NC)
                ins = t.matmul(bank[:, :], WxT[:, c], xnT[:, q, c], start=(c == 0), stop=(c == NC - 1))
                if c == NC - 1:
                    ins.then_inc(ready, 1)

            pe.wait_ge(consts_ready, 1)
            pe.wait_ge(consts_loaded, 16 * 8)
            bank, ready = free("pro", 0, "WxT")
            for c in range(NC):
                last = t.transpose(bank[:, c * 96:(c + 1) * 96], Wx_in[:, c * P:(c + 1) * P], ident[0:96, 0:96])
            last.then_inc(ready, 1)
            bank, ready = free("pro", 0, "WdtT")
            for c in range(NC):
                last = t.transpose(bank[0:RANK, c * P:(c + 1) * P], Wdt_in[:, c], ident[:, :])
            last.then_inc(ready, 1)
            for c in range(NC):
                bank, ready = free("pro", 0, f"wT{c}")
                for j in range(NC):
                    last = t.transpose(bank[:, j * P:(j + 1) * P], w_in[:, j, c * P:(c + 1) * P], ident[:, :])
                last.then_inc(ready, 1)
            bank, ready = free("pro", 0, "amaxT")
            pe.wait_ge(amax_ready, 1)
            t.transpose(bank[0:2, 0:P], amax2[:, 0:2], ident[:, :]).then_inc(ready, 1)
            bank, ready = free("pro", 0, "amaxB")
            pe.wait_ge(amax_row, 1)
            t.matmul(bank[:, 0:2], ones[0:2, :], amax2[0:2, 6:8], start=True, stop=True).then_inc(ready, 1)
            for name in PROLOGUE[8:]:
                event("pro", 0, name, 0, 0)

            def add_up(K, n, c):
                step = K * NS + n
                if c == 0:
                    pe.wait_ge(prod_done, step + 1)
                if n == 0:
                    wait(pe, y_taken, (K - 1) * NC + c + 1)
                t.matmul(Y[c][:, :], ident[:, :], h[:, n % NH, c], start=(n == 0),
                         stop=(n == NS - 1)).then_inc(sum_done, 1)

            def body(kind, K, q):
                for n in range(NS):
                    for c in range(NC):
                        now = [(name, *{"m": (K, q), "e": (K - 1, 1 - q), "p": (K + 1, 1 - q)}[k])
                               for name, k in events(kind, n, c)]
                        for name, Q, r in now:
                            if parts(name)[0] in EARLY:
                                event(kind, K, name, Q, r)
                        if n not in DIRECT:
                            s = TURNED.index(n)
                            if c == 0:
                                pe.wait_ge(bT_ready, K * NT + s + 1)
                            if c >= 2:
                                before = K * (NS * NC) + n * NC + c - 2
                            elif s:
                                before = K * (NS * NC) + TURNED[s - 1] * NC + c + 2
                            else:
                                before = (K - 1) * (NS * NC) + TURNED[-1] * NC + c + 2
                            wait(pe, scan_done, before + 1)
                            for j in range(NC):
                                last = t.transpose(BP[c % 2][:, j * P:(j + 1) * P],
                                                   bT[:, s % 2, j, c * P:(c + 1) * P], ident[:, :])
                            last.then_inc(b_ready, 1)
                        if n >= LAG:
                            add_up(K, n - LAG, c)
                        elif kind != "first":
                            add_up(K - 1, n - LAG + NS, c)
                        for name, Q, r in now:
                            if parts(name)[0] not in EARLY:
                                event(kind, K, name, Q, r)
                        if kind != "last":
                            for block in range(NC):
                                if DBL[block] == (n, c):
                                    projection(kind, K, K + 1, 1 - q, block)

            for_chunks(pe, body)
            for n in range(NS - LAG, NS):
                for c in range(NC):
                    add_up(chunks - 1, n, c)
            for name in EPILOGUE:
                event("epi", 0, name, chunks - 1, 1)


_INS = ["L0_attn_u", "L0_attn_W_x", "L0_attn_W_dt", "L0_attn_b_dt", "L0_attn_log_A", "L0_attn_D_param",
        "L0_ffn_weight", "L0_ffn_bias"]


def kernel(**inputs):
    import numpy as _np
    import concourse.bacc as _bacc
    from concourse import mybir as _mybir
    from concourse.bass_utils import run_bass_kernel_spmd as _run

    nc = _bacc.Bacc("TRN2", target_bir_lowering=False, num_devices=1)
    arrays, args = {}, []
    for name in _INS:
        a = _np.ascontiguousarray(inputs[name])
        arrays[f"in_{name}"] = a
        args.append(nc.dram_tensor(f"in_{name}", a.shape, _mybir.dt.from_np(a.dtype), kind="ExternalInput").ap())
    shape = inputs["L0_attn_u"].shape
    out = nc.dram_tensor("out_0", shape, _mybir.dt.float32, kind="ExternalOutput").ap()
    build(nc, *args, out)
    r = _run(nc, [arrays], core_ids=[0])
    return r.results[0]["out_0"]
```
